# Optimizing a Trainium2 kernel written in Bass

```python
import numpy as np
import jax
import jax.numpy as jnp

def _softmax(x, axis=-1):
    return jax.nn.softmax(x, axis=axis)

def _gelu(x):
    return jax.nn.gelu(x, approximate=True)

def _silu(x):
    return jax.nn.silu(x)

def _sigmoid(x):
    return jax.nn.sigmoid(x)

def _layernorm(x, axis=-1, eps=1e-05):
    m = jnp.mean(x, axis=axis, keepdims=True)
    v = jnp.var(x, axis=axis, keepdims=True)
    return (x - m) / jnp.sqrt(v + eps)

def _scatter_add(tgt, idx, src, axis=0):
    return tgt.at[idx].add(src)

def _segment_sum(src, seg, n):
    return jax.ops.segment_sum(src, seg, n)
kernel_name = 'mk_macaron_d1_jaxref_r4_4761e6'

def setup_inputs(seed: int=0):
    np.random.seed(seed)
    _w = jnp.asarray

    def _L0_attn_setup():
        import jax, jax.numpy as jnp
        import numpy as np
        H = 256
        B_SZ = 4
        L = 512
        key = jax.random.key(seed)
        ks = jax.random.split(key, 7)
        s_in = 1.0 / np.sqrt(H)
        x = jax.random.normal(ks[0], (B_SZ, L, H), dtype=jnp.float32)
        W_proj = jax.random.uniform(ks[1], (4 * H, H), minval=-s_in, maxval=s_in, dtype=jnp.float32)
        W_delta = jax.random.uniform(ks[2], (H, H), minval=-s_in, maxval=s_in, dtype=jnp.float32)
        b_delta = jax.random.uniform(ks[3], (H,), minval=-s_in, maxval=s_in, dtype=jnp.float32)
        A = 0.02 * jax.random.normal(ks[4], (1, 1, H), dtype=jnp.float32)
        Bp = 0.02 * jax.random.normal(ks[5], (1, H, 1), dtype=jnp.float32)
        D = jnp.ones((1,), dtype=jnp.float32)
        return {'x': x, 'W_proj': W_proj, 'A': A, 'Bp': Bp, 'D': D, 'W_delta': W_delta, 'b_delta': b_delta}
    _L0_attn_in = _L0_attn_setup()

    def _L0_ffn_setup():
        import math
        import jax, jax.numpy as jnp
        import numpy as np
        CAPACITY_FACTOR = 1.25
        key = jax.random.key(seed)
        ks = jax.random.split(key, 5)
        B, S, H, F, E = (4, 1024, 256, 256, 32)
        scale_in = 1.0 / math.sqrt(H)
        scale_mid = 1.0 / math.sqrt(F)
        return {'x': jax.random.normal(ks[0], (B, S, H), dtype=jnp.float32), 'w_router': jax.random.normal(ks[1], (H, E), dtype=jnp.float32) * scale_in, 'w_gate': jax.random.normal(ks[2], (E, H, F), dtype=jnp.float32) * scale_in, 'w_up': jax.random.normal(ks[3], (E, H, F), dtype=jnp.float32) * scale_in, 'w_down': jax.random.normal(ks[4], (E, F, H), dtype=jnp.float32) * scale_mid}
    _L0_ffn_in = _L0_ffn_setup()
    _d = {'L0_attn_x': _L0_attn_in['x'], 'L0_attn_W_proj': _L0_attn_in['W_proj'], 'L0_attn_A': _L0_attn_in['A'], 'L0_attn_Bp': _L0_attn_in['Bp'], 'L0_attn_D': _L0_attn_in['D'], 'L0_attn_W_delta': _L0_attn_in['W_delta'], 'L0_attn_b_delta': _L0_attn_in['b_delta'], 'L0_ffn_w_router': _L0_ffn_in['w_router'], 'L0_ffn_w_gate': _L0_ffn_in['w_gate'], 'L0_ffn_w_up': _L0_ffn_in['w_up'], 'L0_ffn_w_down': _L0_ffn_in['w_down']}
    _x0 = _d['L0_attn_x']
    _d['L0_attn_x'] = jax.random.normal(jax.random.fold_in(jax.random.key(seed), 1), (8, 2048, 256), dtype=_x0.dtype)
    del _x0
    return _d

def reference(L0_attn_x, L0_attn_W_proj, L0_attn_A, L0_attn_Bp, L0_attn_D, L0_attn_W_delta, L0_attn_b_delta, L0_ffn_w_router, L0_ffn_w_gate, L0_ffn_w_up, L0_ffn_w_down):

    def _L0_attn_ref(x, W_proj, A, Bp, D, W_delta, b_delta):
        import jax, jax.numpy as jnp
        import numpy as np
        H = 256
        B_SZ = 4
        L = 512
        h = x.shape[-1]
        proj = x @ W_proj.T
        delta, Bs, Cs, residual = jnp.split(proj, 4, axis=-1)
        delta = jax.nn.softplus(delta @ W_delta.T + b_delta)
        A1 = A[0, 0]
        B1 = Bp[0, :, 0]
        dA = jnp.exp(delta * A1) * B1
        dB = jnp.cumsum(delta * B1, axis=1)
        uC = jnp.sum(x * Cs, axis=1, keepdims=True)
        Csum = jnp.sum(Cs, axis=1, keepdims=True)
        y = dA * uC + dB * Csum
        return y + residual * D

    def _L0_ffn_ref(x, w_router, w_gate, w_up, w_down):
        import math
        import jax, jax.numpy as jnp
        import numpy as np
        CAPACITY_FACTOR = 1.25
        B, S, H = x.shape
        E = w_gate.shape[0]
        T = B * S
        C = int(math.ceil(CAPACITY_FACTOR * T / E))
        xt = x.reshape(T, H)
        logits = xt @ w_router
        probs = jax.nn.softmax(logits, axis=-1)
        top1 = jnp.argmax(probs, axis=-1)
        gate = jnp.take_along_axis(probs, top1[:, None], axis=1)[:, 0]
        onehot = jax.nn.one_hot(top1, E, dtype=jnp.int32)
        pos = jnp.cumsum(onehot, axis=0)[jnp.arange(T), top1] - 1
        accepted = pos < C
        slot = jnp.where(accepted, top1 * C + pos, E * C)
        buf = jnp.zeros((E * C + 1, H), dtype=x.dtype).at[slot].set(xt)
        buf = buf[:E * C].reshape(E, C, H)
        g = jnp.einsum('ech,ehf->ecf', buf, w_gate)
        u = jnp.einsum('ech,ehf->ecf', buf, w_up)
        y = jnp.einsum('ecf,efh->ech', jax.nn.silu(g) * u, w_down)
        out_tok = y.reshape(E * C, H)[jnp.clip(slot, 0, E * C - 1)]
        out_tok = jnp.where(accepted[:, None], out_tok * gate[:, None], 0.0)
        return (xt + out_tok).reshape(B, S, H)
    x = L0_attn_x
    x = x + 0.5 * _L0_ffn_ref(_layernorm(x, axis=-1), L0_ffn_w_router, L0_ffn_w_gate, L0_ffn_w_up, L0_ffn_w_down)
    x = x + _L0_attn_ref(_layernorm(x, axis=-1), L0_attn_W_proj, L0_attn_A, L0_attn_Bp, L0_attn_D, L0_attn_W_delta, L0_attn_b_delta)
    x = x + 0.5 * _L0_ffn_ref(_layernorm(x, axis=-1), L0_ffn_w_router, L0_ffn_w_gate, L0_ffn_w_up, L0_ffn_w_down)
    return x

_drawn_inputs = setup_inputs


def setup_inputs(seed=0):
    import zlib

    import numpy as np

    out = dict(_drawn_inputs(seed))
    spreads = {}
    factors = {}
    for name, (base, spread) in spreads.items():
        noise = np.random.default_rng([zlib.crc32(name.encode()), seed]).standard_normal(out[name].shape)
        drawn = base * np.exp(spread * noise) if base else spread * noise
        out[name] = jnp.asarray(drawn.astype(out[name].dtype))
    for name, factor in factors.items():
        out[name] = (out[name] * factor).astype(out[name].dtype)
    return out
```

```python
from contextlib import ExitStack

import concourse.bass as bass
from concourse import mybir

ALU = mybir.AluOpType
ACT = mybir.ActivationFunctionType
AX = mybir.AxisListType.X
F32 = mybir.dt.float32
F32R = mybir.dt.float32r
BF16 = mybir.dt.bfloat16
U32 = mybir.dt.uint32

P = 128
H = 256
HC = H // P
E = 32
F = 256
BATCH, SEQ = 8, 2048
T = BATCH * SEQ
NT = T // P
TB = SEQ // P
CAP = -(-5 * T // (4 * E))
ET = CAP // P
ST = E * ET
DROP = E * CAP
CH = 2
NC = TB // CH
CT = CH * P
EPS = 1e-5
SL = CAP // 2
assert CAP % P == 0 and SL >= 256 and SL <= 512


PASSED = {}


def apart(eng):
    eng.sem_inc(PASSED[eng.engine], 1)


class Count:

    def __init__(self, sem, per, credit=0):
        self.sem, self.per, self.credit = sem, per, credit

    def wait(self, eng, turn, n):
        assert n + self.credit >= 1
        eng.wait_ge(self.sem, turn * self.per + (n + self.credit))

    def wait_apart(self, eng, turn, n):
        self.wait(eng, turn, n)
        apart(eng)

    def grant(self, eng):
        eng.sem_inc(self.sem, self.credit)


class Chain:

    def __init__(self, sem, per):
        self.sem, self.per = sem, per
        self.turn, self.n = 0, 0

    def begin(self, turn):
        self.turn, self.n = turn, 0

    def link(self, eng, ins, alone=False):
        self.n += 1
        ins.then_inc(self.sem, 1)
        eng.wait_ge(self.sem, self.turn * self.per + self.n)
        if alone:
            apart(eng)

    def end(self):
        assert self.n == self.per, (self.n, self.per)


def macaron(nc, x, w_proj0, w_delta_t, w_c, w_c_t, w_r_t, a_vec, b_vec, d_vec, b_delta,
            w_router, w_gate, w_up, w_down, c_f32, c_bf16, out):
    with ExitStack() as ctx:
        names = [0]

        def sb(shape, dt=F32, stack=ctx, name="t"):
            names[0] += 1
            return stack.enter_context(nc.sbuf_tensor(f"{name}_{names[0]}", shape, dt))

        def sem(name):
            names[0] += 1
            return ctx.enter_context(nc.semaphore(f"{name}_{names[0]}"))

        def count(name, per, credit=0):
            return Count(sem(name), per, credit)

        for eng in (nc.vector, nc.scalar, nc.gpsimd):
            PASSED[eng.engine] = sem("passed")

        xn_rows = nc.dram_tensor("xn_rows", [T, H], F32, kind="Internal").ap()
        y_rows = nc.dram_tensor("y_rows", [DROP + P, H], F32, kind="Internal").ap()
        w_ready = nc.dram_tensor("w_ready", [P, 8 * H], F32, kind="Internal").ap()

        ps = ctx.enter_context(nc.psum_tensor("ps", [P, 8, 512], F32))

        X = sb([P, NT, H], name="x")
        RSTD = sb([P, NT], name="rstd")
        NMR = sb([P, NT], name="nmr")
        GATE = sb([P, NT], name="gate")
        SLOT = sb([P, NT], U32, name="slot")
        INV = sb([P, ST], U32, name="inv")
        CF = sb([P, 128 + 32 + 1 + 16 + CH], F32, name="cf")
        CB = sb([P, 128 * 3 + 160 + 128], BF16, name="cb")
        WR = sb([P, HC, E], F32, name="wr")
        IDENT = CF[:, 0:128]
        REV = CF[:, 128:160]
        LANE = CF[:, 160:161]
        IOTA16 = CF[:, 161:177]
        NHALF = CF[:, 177:177 + CH]
        TRI = CB[:, 0:128]
        ONES = CB[:, 128:256]
        IOTA128 = CB[:, 256:384]
        IOTA160 = CB[:, 384:544]
        BZERO = CB[:, 544:672]
        sbuf_base = [0]

        def mid(ap, n):
            return ap.unsqueeze(1).to_broadcast([P, n, ap.shape[1]])

        def last(ap, k):
            return ap.unsqueeze(2).to_broadcast([P, ap.shape[1], k])

        class Tail:

            def __init__(self, stack, tag, banks, n_t, xr):
                self.bt, self.bl, self.bc, self.bi = banks
                self.n_t, self.xr = n_t, xr
                s = lambda shape, dt=F32, name="r": sb(shape, dt, stack, name)
                self.bs = s([P, 2, CH, 6])
                self.mv = s([P, 2, CH, 2])
                self.rb = s([P, TB])
                self.nb = s([P, TB])
                self.mr = s([P, CH])
                self.ve = s([P, CH])
                self.xn = s([P, xr, CH, H])
                self.xt = s([P, 2, HC, CH, P])
                self.d = s([P, TB, E])
                self.ex = s([P, TB, E])
                self.cand = s([P, TB, E])
                self.oh = s([P, TB, E], BF16)
                self.small = s([P, 12, TB])
                self.slu = s([P, 3, TB], U32)
                self.carry = s([P, E], BF16)
                self.cr = s([P, E])
                self.oa = s([P, 2, 4, P], BF16)
                self.ob = s([P, 2, 4, 2, ST], BF16)
                self.inv_f = s([P, ST])
                self.inv_g = s([P, ST])
                self.stats = count(f"{tag}_stats", NC)
                self.rdone = count(f"{tag}_rstd", NC, 2)
                self.kept = count(f"{tag}_kept", 1, 1)
                self.normed = count(f"{tag}_normed", NC, 1)
                self.st = [sem(f"{tag}_rows_stored{k}") for k in range(xr)]
                self.free = count(f"{tag}_rows_free", NC, xr)
                self.turned = count(f"{tag}_turned", NC, xr)
                self.evac = count(f"{tag}_evac", NC, n_t)
                self.logits = count(f"{tag}_logits", NC, 2)
                self.lread = count(f"{tag}_logits_read", 1, 1)
                self.expd = count(f"{tag}_exp", 1)
                self.ohd = count(f"{tag}_onehot", 1)
                self.cnt = count(f"{tag}_count", 1)
                self.hot = count(f"{tag}_hot", 4)
                self.inv = count(f"{tag}_inv", 4, 2)
                self.fin = sem(f"{tag}_inv_fin")
                self.dch = Chain(sem(f"{tag}_dve"), NC)
                self.pch = Chain(sem(f"{tag}_pool"), 3 * NC)
                self.post_ch = Chain(sem(f"{tag}_post"), 18)
                self.setup_done = sem(f"{tag}_setup")

            def dve_setup(self):
                nc.vector.memset(self.carry[:], 0.0)
                nc.vector.tensor_scalar(self.small[:, 11, :], IOTA16, float(-TB), None,
                                        ALU.add).then_inc(self.setup_done, 1)
                nc.vector.wait_ge(self.setup_done, 1)
                self.lread.grant(nc.vector)
                self.kept.grant(nc.vector)

            def dve_stats(self, dve, t, c):
                if c == 0:
                    self.dch.begin(t)
                self.rdone.wait_apart(dve, t, c - 1)
                for j in range(CH):
                    ins = dve.bn_stats(self.bs[:, c % 2, j, :], X[:, TB * t + (CH * c + j), :])
                self.dch.link(dve, ins, alone=True)
                for j in range(CH):
                    ins = dve.bn_aggr(self.mv[:, c % 2, j, :], self.bs[:, c % 2, j, :])
                ins.then_inc(self.stats.sem, 1)

            def dve_keep(self, dve, t):
                self.rdone.wait_apart(dve, t, NC)
                dve.tensor_copy(RSTD[:, bass.ds(TB * t, TB)], self.rb[:])
                dve.tensor_copy(NMR[:, bass.ds(TB * t, TB)], self.nb[:]).then_inc(self.kept.sem, 1)
                self.dch.end()

            def pool_setup(self):
                self.rdone.grant(nc.gpsimd)

            def pool_rstd(self, pool, t, c):
                if c == 0:
                    self.pch.begin(t)
                    self.kept.wait(pool, t, 0)
                    self.normed.wait(pool, t, 0)
                self.stats.wait_apart(pool, t, c + 1)
                rb = self.rb[:, CH * c:CH * c + CH]
                nb = self.nb[:, CH * c:CH * c + CH]
                mean, var = self.mv[:, c % 2, :, 0], self.mv[:, c % 2, :, 1]
                self.pch.link(pool, nc.gpsimd.tensor_scalar(self.ve[:], var, EPS, None, ALU.add))
                self.pch.link(pool, nc.gpsimd.tensor_tensor(rb, self.ve[:], NHALF, ALU.pow))
                self.pch.link(pool, nc.gpsimd.tensor_tensor(self.mr[:], mean, rb, ALU.mult), alone=True)
                nc.gpsimd.tensor_scalar(nb, self.mr[:], -1.0, None, ALU.mult).then_inc(self.rdone.sem, 1)
                if c == NC - 1:
                    self.pch.end()

            def act_setup(self, act):
                self.evac.grant(act)
                self.normed.grant(act)

            def act_norm(self, act, t, c):
                self.free.wait(act, t, c + 1 - self.xr)
                self.turned.wait(act, t, c + 1 - self.xr)
                self.rdone.wait_apart(act, t, c + 1)
                for j in range(CH):
                    k = CH * c + j
                    ins = act.activation(self.xn[:, c % self.xr, j, :], X[:, TB * t + k, :], ACT.Identity,
                                         bias=self.nb[:, k:k + 1], scale=self.rb[:, k:k + 1])
                ins.then_inc(self.normed.sem, 1)

            def act_evac(self, act, t, c):
                self.turned.wait(act, t, c + 1)
                self.logits.wait(act, t, c - 1)
                act.copy(self.xt[:, c % 2].rearrange("p a b c -> p (a b c)"),
                         ps[:, self.bt + c % self.n_t, :]).then_inc(self.evac.sem, 1)

            def act_exp(self, act, p):
                self.post_ch_wait(act, p, 2)
                act.activation(self.ex[:], self.d[:], ACT.Exp).then_inc(self.expd.sem, 1)

            def post_ch_wait(self, eng, p, n):
                eng.wait_ge(self.post_ch.sem, p * self.post_ch.per + n)

            def sp_setup(self):
                self.free.grant(nc.sync)

            def sp_free(self, sp, t, c):
                sp.wait_ge(self.st[c % self.xr], t * (16 * NC // self.xr) + 16 * (c // self.xr + 1))
                sp.sem_inc(self.free.sem, 1)

            def sp_store(self, sp, t, c):
                self.normed.wait(sp, t, c + 1)
                rows = xn_rows.rearrange("(k j p) d -> k p j d", p=P, j=CH)
                sp.dma_start(rows[t * NC + c], self.xn[:, c % self.xr]).then_inc(self.st[c % self.xr], 16)
                lag = self.xr // 2
                if c >= lag:
                    self.sp_free(sp, t, c - lag)
                if c == NC - 1:
                    for k in range(NC - lag, NC):
                        self.sp_free(sp, t, k)

            def pe_setup(self, pe):
                self.turned.grant(pe)
                self.evac_n = 0
                self.logits.grant(pe)
                self.inv.grant(pe)
                for k in range(2):
                    pe.matmul(ps[:, self.bi, ST * k:ST * k + ST], BZERO, IOTA160, start=(k == 0), stop=False,
                              skip_group_check=True)

            def pe_turn(self, pe, t, c):
                self.normed.wait(pe, t, c + 1)
                self.evac.wait(pe, t, c + 1 - self.n_t)
                for j in range(CH):
                    for h in range(HC):
                        o = (h * CH + j) * P
                        ins = pe.transpose(ps[:, self.bt + c % self.n_t, o:o + P],
                                           self.xn[:, c % self.xr, j, h * P:(h + 1) * P], IDENT)
                ins.then_inc(self.turned.sem, 1)

            def pe_logits(self, pe, t, c):
                self.evac.wait(pe, t, c + 1)
                if c == 0:
                    self.lread.wait(pe, t, 0)
                for j in range(CH):
                    k = CH * c + j
                    for h in range(HC):
                        ins = pe.matmul(ps[:, self.bl, k * E:(k + 1) * E], self.xt[:, c % 2, h, j, :],
                                        WR[:, h, :], start=(h == 0), stop=(h == HC - 1))
                ins.then_inc(self.logits.sem, 1)

            def post(self, dve, p, step):
                ch, s = self.post_ch, self.small
                lg = ps[:, self.bl, :].rearrange("p (t e) -> p t e", e=E)
                ct = ps[:, self.bc, :].rearrange("p (t e) -> p t e", e=E)
                mx, rr, se, gt, ci, acc, t1, t2, slf, lo, hi, tid = (s[:, k, :] for k in range(12))
                if step == 0:
                    ch.begin(p)
                    self.logits.wait(dve, p, NC)
                    ch.link(dve, dve.reduce_max(mx, lg, AX))
                    ch.link(dve, dve.tensor_tensor(self.d[:], lg, last(mx, E), ALU.subtract))
                    dve.sem_inc(self.lread.sem, 1)
                    ch.link(dve, dve.scalar_tensor_tensor(self.cand[:], self.d[:], 0.0, mid(REV, TB), ALU.is_ge,
                                                          ALU.mult))
                    ch.link(dve, dve.reduce_max(rr, self.cand[:], AX))
                    dve.tensor_tensor(self.oh[:], mid(REV, TB), last(rr, E), ALU.is_equal).then_inc(self.ohd.sem, 1)
                if step == 1:
                    self.expd.wait(dve, p, 1)
                    ch.link(dve, dve.reduce_sum(se, self.ex[:], AX))
                    ch.link(dve, dve.reciprocal(gt, se))
                if step == 2:
                    self.cnt.wait(dve, p, 1)
                    ch.link(dve, dve.tensor_tensor(self.cand[:], self.oh[:], ct, ALU.mult))
                    ch.link(dve, dve.reduce_sum(ci, self.cand[:], AX))
                    ch.link(dve, dve.reduce_sum(self.cr[:], self.oh[:].rearrange("p t e -> p e t"), AX))
                    ch.link(dve, dve.tensor_tensor(self.carry[:], self.carry[:], self.cr[:], ALU.add))
                    ch.link(dve, dve.tensor_scalar(acc, ci, float(CAP), None, ALU.is_le))
                    ch.link(dve, dve.scalar_tensor_tensor(t1, rr, float(-CAP), ci, ALU.mult, ALU.add))
                    ch.link(dve, dve.scalar_tensor_tensor(t2, t1, -1.0, acc, ALU.add, ALU.mult))
                    ch.link(dve, dve.tensor_scalar(slf, t2, float(DROP), None, ALU.add))
                    ch.link(dve, dve.tensor_copy(self.slu[:, 0, :], slf), alone=True)
                    dve.tensor_copy(SLOT[:, bass.ds(TB * p, TB)], self.slu[:, 0, :])
                    dve.tensor_scalar(self.slu[:, 1, :], self.slu[:, 0, :], P - 1, None, ALU.bitwise_and)
                    ch.link(dve, dve.tensor_scalar(self.slu[:, 2, :], self.slu[:, 0, :], 7, None,
                                                   ALU.logical_shift_right))
                    dve.tensor_copy(lo, self.slu[:, 1, :])
                    dve.tensor_copy(hi, self.slu[:, 2, :])
                    dve.tensor_scalar(tid, tid, float(TB), None, ALU.add)
                    ch.link(dve, dve.scalar_tensor_tensor(GATE[:, bass.ds(TB * p, TB)], gt, 0.5, acc,
                                                          ALU.mult, ALU.mult))
                if step >= 3:
                    q = step - 3
                    self.inv.wait(dve, p, q + 1 - 2)
                    for k in range(4):
                        j = 4 * q + k
                        dve.tensor_scalar(self.oa[:, q % 2, k, :], IOTA128, lo[:, j:j + 1], None, ALU.is_equal)
                        dve.tensor_scalar(self.ob[:, q % 2, k, 0, :], IOTA160, hi[:, j:j + 1], tid[:, j:j + 1],
                                          ALU.is_equal, ALU.mult)
                        ins = dve.tensor_scalar(self.ob[:, q % 2, k, 1, :], IOTA160, hi[:, j:j + 1], LANE,
                                                ALU.is_equal, ALU.mult)
                    ins.then_inc(self.hot.sem, 1)
                if step == 6:
                    self.hot.wait(dve, p, 4)
                    dve.sem_inc(ch.sem, 1)
                    ch.n += 1
                    ch.end()

            def pe_count(self, pe, p):
                self.ohd.wait(pe, p, 1)
                ct = ps[:, self.bc, :].rearrange("p (t e) -> p t e", e=E)
                pe.matmul(ct, ONES, mid(self.carry[:], TB), start=True, stop=False, skip_group_check=True)
                for j in range(TB - 1):
                    pe.matmul(ct[:, j + 1:, :], ONES, mid(self.oh[:, j, :], TB - 1 - j), start=False, stop=False,
                              skip_group_check=True)
                pe.matmul(ct, TRI, self.oh[:], start=False, stop=True,
                          skip_group_check=True).then_inc(self.cnt.sem, 1)

            def pe_inv(self, pe, p, q):
                self.hot.wait(pe, p, q + 1)
                for k in range(4):
                    ins = pe.matmul(ps[:, self.bi, 0:2 * ST], self.oa[:, q % 2, k, :], self.ob[:, q % 2, k],
                                    start=False, stop=False, skip_group_check=True)
                ins.then_inc(self.inv.sem, 1)

            def pe_finish(self, pe):
                for k in range(2):
                    ins = pe.matmul(ps[:, self.bi, ST * k:ST * k + ST], BZERO, IOTA160, start=False,
                                    stop=(k == 1), skip_group_check=True)
                ins.then_inc(self.fin, 1)

            def dve_finish(self, dve):
                dve.wait_ge(self.fin, 1)
                dve.tensor_copy(self.inv_f[:], ps[:, self.bi, ST:2 * ST]).then_inc(self.fin, 1)
                dve.wait_ge(self.fin, 2)
                dve.scalar_tensor_tensor(self.inv_g[:], ps[:, self.bi, 0:ST], float(P), self.inv_f[:],
                                         ALU.mult, ALU.add).then_inc(self.fin, 1)
                dve.wait_ge(self.fin, 3)
                dve.tensor_copy(INV[:], self.inv_g[:])

        with ExitStack() as st:
            tail = Tail(st, "p1", (0, 2, 3, 4), 2, 4)
            s_const = sem("const_in")
            s_x = [sem(f"x_in{g}") for g in range(4)]
            s_w = sem("w_in")
            s_prep, s_prepd, s_wout = sem("prep"), sem("prep_done"), sem("w_out")
            s_zero, s_zout = sem("zero"), sem("zero_out")
            WIN = sb([P, 6, H], F32, st, "win")
            WOUT = sb([P, 8, H], F32R, st, "wout")
            DV = sb([P, 1], F32, st, "dv")
            WT = sb([P, 2, H], F32, st, "wt")
            zero = sb([P, H], F32, st, "zero")
            block = st.enter_context(nc.Block())
            x_in = x.rearrange("(b g j p) d -> b g p j d", p=P, j=4, g=4)

            def load(sp, b, g):
                sp.dma_start(X[:, bass.ds(TB * b + 4 * g, 4), :], x_in[b, g]).then_inc(s_x[g], 16)

            @block.sync
            def _(sp):
                tail.sp_setup()
                sp.dma_start(CF[:], c_f32).then_inc(s_const, 16)
                sp.dma_start(CB[:], c_bf16).then_inc(s_const, 16)
                sp.dma_start(WR[:], w_router.rearrange("(a p) e -> p a e", p=P)).then_inc(s_const, 16)
                for g in range(4):
                    load(sp, 0, g)
                for k, w in enumerate((w_proj0, w_delta_t, w_r_t)):
                    sp.dma_start(WIN[:, 2 * k:2 * k + 2, :], w.rearrange("(a p) e -> p a e", p=P)).then_inc(s_w, 16)
                sp.dma_start(DV[:], d_vec.to_broadcast([P, 1])).then_inc(s_w, 16)
                sp.wait_ge(s_zero, 1)
                sp.dma_start(y_rows[DROP:DROP + P, :], zero[:]).then_inc(s_zout, 16)

                def turn(t, more):
                    for c in range(NC):
                        if more and c % 2 == 0:
                            tail.stats.wait(sp, t, c + 2)
                            load(sp, t + 1, c // 2)
                        tail.sp_store(sp, t, c)

                with sp.Fori(0, BATCH - 1) as b:
                    turn(b, True)
                turn(BATCH - 1, False)
                sp.wait_ge(s_prepd, 5)
                sp.dma_start(w_ready, WOUT[:].bitcast(F32).rearrange("p a b -> p (a b)")).then_inc(s_wout, 16)
                sp.wait_ge(s_wout, 16)
                sp.wait_ge(s_zout, 16)

            @block.gpsimd
            def _(pool):
                tail.pool_setup()
                nc.gpsimd.memset(zero[:], 0.0).then_inc(s_zero, 1)
                with pool.Fori(0, BATCH) as b:
                    for c in range(NC):
                        tail.pool_rstd(pool, b, c)

            @block.scalar
            def _(act):
                tail.act_setup(act)

                def turn(t, post):
                    for c in range(NC + 1):
                        if c == 1 and post is not None:
                            tail.act_exp(act, post)
                        if c < NC:
                            tail.act_norm(act, t, c)
                        if c >= 1:
                            tail.act_evac(act, t, c - 1)

                turn(0, None)
                with act.Fori(0, BATCH - 1) as b:
                    turn(b + 1, b)
                tail.act_exp(act, BATCH - 1)

            @block.vector
            def _(dve):
                dve.wait_ge(s_const, 48)
                tail.dve_setup()

                def turn(t, post):
                    for c in range(NC):
                        if c % 2 == 0:
                            dve.wait_ge(s_x[c // 2], t * 16 + 16)
                        tail.dve_stats(dve, t, c)
                        if post is not None and c < 7:
                            tail.post(dve, post, c)
                    tail.dve_keep(dve, t)

                turn(0, None)
                dve.wait_ge(s_prep, 1)
                dve.tensor_copy(WT[:], ps[:, 5, :].rearrange("p (a b) -> p a b", a=2)).then_inc(s_prepd, 1)
                dve.tensor_scalar(WIN[:, 4:6, :], WIN[:, 4:6, :], DV[:, 0:1], None, ALU.mult).then_inc(s_prepd, 1)
                dve.wait_ge(s_prepd, 2)
                dve.tensor_copy(WOUT[:, 0:2, :], WT[:])
                dve.tensor_copy(WOUT[:, 4:6, :], WIN[:, 4:6, :]).then_inc(s_prepd, 1)
                dve.wait_ge(s_prepd, 3)
                dve.tensor_tensor(WOUT[:, 2:4, :], WT[:], WOUT[:, 0:2, :].bitcast(F32), ALU.subtract).then_inc(s_prepd, 1)
                dve.tensor_tensor(WOUT[:, 6:8, :], WIN[:, 4:6, :], WOUT[:, 4:6, :].bitcast(F32),
                                  ALU.subtract).then_inc(s_prepd, 1)
                with dve.Fori(0, BATCH - 1) as b:
                    turn(b + 1, b)
                for k in range(7):
                    tail.post(dve, BATCH - 1, k)
                tail.dve_finish(dve)

            @block.tensor
            def _(pe):
                pe.wait_ge(s_const, 48)
                tail.pe_setup(pe)
                pe.wait_ge(s_w, 64)
                for kh in range(HC):
                    for j in range(HC):
                        ins = pe.matmul(ps[:, 5, kh * H:(kh + 1) * H], WIN[:, j, kh * P:(kh + 1) * P], WIN[:, 2 + j, :],
                                        start=(j == 0), stop=(j == HC - 1))
                ins.then_inc(s_prep, 1)

                def turn(t, post):
                    for c in range(NC + 1):
                        if c < NC:
                            tail.pe_turn(pe, t, c)
                        if c >= 1:
                            tail.pe_logits(pe, t, c - 1)
                        if post is not None:
                            if c == 1:
                                tail.pe_count(pe, post)
                            if c >= 4 and c < 8:
                                tail.pe_inv(pe, post, c - 4)

                turn(0, None)
                with pe.Fori(0, BATCH - 1) as b:
                    turn(b + 1, b)
                tail.pe_count(pe, BATCH - 1)
                for q in range(4):
                    tail.pe_inv(pe, BATCH - 1, q)
                tail.pe_finish(pe)

        def experts(tag):
            with ExitStack() as st:
                NQ = (ET + 1) // 2
                WRAW = sb([P, 6, F], F32, st, "wraw")
                WS = sb([P, 2, 2, 6, F], F32R, st, "ws")
                IDX = sb([P, 2, ET], U32, st, "idx")
                XG = sb([P, 2, ET, H], F32, st, "xg")
                XS = sb([P, 2, HC, CAP], F32R, st, "xs")
                SG = sb([P, 2, SL], F32, st, "sg")
                HF = sb([P, 2, SL], F32, st, "hf")
                HS = sb([P, 2, HC, CAP], F32R, st, "hs")
                YS = sb([P, ET, H], F32, st, "ys")
                w_in = [sem(f"{tag}_w_in")]
                xg_in = [sem(f"{tag}_xg_in{r}") for r in range(2)]
                y_out = sem(f"{tag}_y_out")
                whi = count(f"{tag}_whi", 1)
                wlo = count(f"{tag}_wlo", 1, 1)
                idx = count(f"{tag}_idx", 1)
                turned = count(f"{tag}_turned", NQ, 2 * NQ)
                xhi = count(f"{tag}_xhi", NQ)
                xlo = count(f"{tag}_xlo", NQ, 2)
                gu = count(f"{tag}_gu", 4, 4)
                silu = count(f"{tag}_silu", 4)
                hm = count(f"{tag}_h", 4, 2)
                hhi = count(f"{tag}_hhi", 4)
                hlo = count(f"{tag}_hlo", 4, 2)
                yd = count(f"{tag}_y", NQ, 2 * NQ)
                ycp = count(f"{tag}_ycopy", NQ, 2)
                yfree = count(f"{tag}_yfree", 1, 1)
                block = st.enter_context(nc.Block())
                widths = [min(2, ET - 2 * q) * P for q in range(NQ)]

                def loop(eng, body, first=None):
                    with eng.Fori(0, E // 2 - 1) as i:
                        body(i * 2, 0, True)
                        body(i * 2 + 1, 1, True)
                    body(E - 2, 0, True)
                    body(E - 1, 1, False)

                @block.sync
                def _(sp):
                    yfree.grant(sp)
                    views = [w.rearrange("e (a p) f -> e p a f", p=P) for w in (w_gate, w_up, w_down)]

                    def weights(e):
                        wlo.wait(sp, e, 0)
                        for k, v in enumerate(views):
                            sp.dma_start(WRAW[:, 2 * k:2 * k + 2, :], v[e]).then_inc(w_in[0], 16)

                    y_out_v = y_rows[0:DROP, :].rearrange("(e t p) d -> e p t d", p=P, t=ET)

                    def body(e, r, more):
                        if more:
                            weights(e + 1)
                        ycp.wait(sp, e, NQ)
                        sp.dma_start(y_out_v[e], YS[:]).then_inc(y_out, 16)
                        sp.wait_ge(y_out, e * 16 + 16)
                        sp.sem_inc(yfree.sem, 1)

                    weights(0)
                    loop(sp, body)

                @block.gpsimd
                def _(pool):
                    def gather(e, r):
                        turned.wait(pool, e, -NQ)
                        idx.wait_apart(pool, e, 1)
                        for k in range(ET):
                            nc.gpsimd.indirect_dma_start(
                                out=XG[:, r, k, :], out_offset=None, in_=xn_rows,
                                in_offset=bass.IndirectOffsetOnAxis(ap=IDX[:, r, k:k + 1], axis=0),
                            ).then_inc(xg_in[r], 16)

                    with pool.Fori(0, E // 2) as i:
                        gather(i * 2, 0)
                        gather(i * 2 + 1, 1)

                @block.scalar
                def _(act):
                    ycp.grant(act)

                    def split_w(e, r):
                        act.wait_ge(w_in[0], e * 48 + 48)
                        yd.wait(act, e, -NQ)
                        act.copy(WS[:, r, 0], WRAW[:]).then_inc(whi.sem, 1)

                    def x_hi(e, q):
                        turned.wait(act, e, q + 1)
                        if q == 0:
                            gu.wait(act, e, 0)
                        o = ps[:, q % 2, :].rearrange("p (a b) -> p a b", a=HC)[:, :, 0:widths[q]]
                        act.copy(XS[:, 0, :, 2 * P * q:2 * P * q + widths[q]], o).then_inc(xhi.sem, 1)

                    def h_hi(e, m):
                        hm.wait(act, e, m + 1)
                        if m == 0:
                            yd.wait(act, e, 0)
                        c, f = divmod(m, 2)
                        act.copy(HS[:, 0, f, SL * c:SL * c + SL], HF[:, m % 2, :]).then_inc(hhi.sem, 1)

                    def body(e, r, more):
                        for m in range(5):
                            if m < 4:
                                gu.wait(act, e, m + 1)
                                hm.wait(act, e, m + 1 - 2)
                                act.activation(SG[:, m % 2, :], ps[:, 2 + 2 * (m % 2), 0:SL],
                                               ACT.Silu).then_inc(silu.sem, 1)
                            if m == 0 and more:
                                split_w(e + 1, 1 - r)
                            if m >= 1:
                                h_hi(e, m - 1)
                        if more:
                            for q in range(NQ):
                                x_hi(e + 1, q)
                        for q in range(NQ):
                            yd.wait(act, e, q + 1)
                            if q == 0:
                                yfree.wait(act, e, 0)
                            act.copy(YS[:, 2 * q:2 * q + widths[q] // P, :],
                                     ps[:, 6 + q % 2, 0:2 * widths[q]].rearrange("p (t d) -> p t d", d=H)
                                     ).then_inc(ycp.sem, 1)

                    split_w(0, 0)
                    for q in range(NQ):
                        x_hi(0, q)
                    loop(act, body)

                @block.vector
                def _(dve):
                    wlo.grant(dve)
                    xlo.grant(dve)
                    hm.grant(dve)
                    hlo.grant(dve)

                    def index(e, r):
                        dve.tensor_copy(IDX[:, r, :], INV[:, bass.ds(e * ET, ET)]).then_inc(idx.sem, 1)

                    def split_w(e, r):
                        whi.wait(dve, e, 1)
                        dve.tensor_tensor(WS[:, r, 1], WRAW[:], WS[:, r, 0].bitcast(F32),
                                          ALU.subtract).then_inc(wlo.sem, 1)

                    def x_lo(e, q):
                        xhi.wait(dve, e, q + 1)
                        o = ps[:, q % 2, :].rearrange("p (a b) -> p a b", a=HC)[:, :, 0:widths[q]]
                        s = slice(2 * P * q, 2 * P * q + widths[q])
                        dve.tensor_tensor(XS[:, 1, :, s], o, XS[:, 0, :, s].bitcast(F32),
                                          ALU.subtract).then_inc(xlo.sem, 1)

                    def h_lo(e, m):
                        hhi.wait(dve, e, m + 1)
                        c, f = divmod(m, 2)
                        s = slice(SL * c, SL * c + SL)
                        dve.tensor_tensor(HS[:, 1, f, s], HF[:, m % 2, :], HS[:, 0, f, s].bitcast(F32),
                                          ALU.subtract).then_inc(hlo.sem, 1)

                    def body(e, r, more):
                        for m in range(5):
                            if m < 4:
                                silu.wait(dve, e, m + 1)
                                hlo.wait(dve, e, m - 1)
                                dve.tensor_tensor(HF[:, m % 2, :], ps[:, 3 + 2 * (m % 2), 0:SL], SG[:, m % 2, :],
                                                  ALU.mult).then_inc(hm.sem, 1)
                            if m == 1 and more:
                                split_w(e + 1, 1 - r)
                            if m >= 1:
                                h_lo(e, m - 1)
                        if more:
                            for q in range(NQ):
                                x_lo(e + 1, q)

                    def gathered(e, r):
                        dve.wait_ge(xg_in[r], e * (8 * ET) + (2 - r) * 8 * ET)
                        apart(dve)

                    index(0, 0)
                    index(1, 1)
                    split_w(0, 0)
                    for q in range(NQ):
                        x_lo(0, q)

                    def pair(i, more):
                        body(i * 2, 0, True)
                        if more:
                            gathered(i * 2, 0)
                            index(i * 2 + 2, 0)
                        body(i * 2 + 1, 1, more)
                        if more:
                            gathered(i * 2 + 1, 1)
                            index(i * 2 + 3, 1)

                    with dve.Fori(0, E // 2 - 1) as i:
                        pair(i, True)
                    pair(E // 2 - 1, False)

                @block.tensor
                def _(pe):
                    turned.grant(pe)
                    gu.grant(pe)
                    yd.grant(pe)

                    def turn(e, r):
                        pe.wait_ge(xg_in[r], e * (8 * ET) + (2 - r) * 8 * ET)
                        for q in range(NQ):
                            xlo.wait(pe, e, q + 1 - 2)
                            for j in range(widths[q] // P):
                                for h in range(HC):
                                    o = h * 2 * P + j * P
                                    ins = pe.transpose(ps[:, q % 2, o:o + P],
                                                       XG[:, r, 2 * q + j, h * P:(h + 1) * P], IDENT)
                            ins.then_inc(turned.sem, 1)

                    def product(dst, left, right):
                        terms = [(a, b, k) for k in range(HC) for a, b in ((0, 0), (0, 1), (1, 0))]
                        for n, (a, b, k) in enumerate(terms):
                            ins = pe.matmul(dst, left(a, k), right(b, k), start=(n == 0), stop=(n == len(terms) - 1))
                        return ins

                    def body(e, r, more):
                        wlo.wait(pe, e, 1)
                        xlo.wait(pe, e, NQ)
                        for m in range(4):
                            c, f = divmod(m, 2)
                            hm.wait(pe, e, m + 1 - 2)
                            for n in range(2):
                                ins = product(
                                    ps[:, 2 + 2 * (m % 2) + n, 0:SL],
                                    lambda a, k: WS[:, r, a, 2 * n + k, f * P:(f + 1) * P],
                                    lambda b, k: XS[:, b, k, SL * c:SL * c + SL],
                                )
                            ins.then_inc(gu.sem, 1)
                        if more:
                            turn(e + 1, 1 - r)
                        hlo.wait(pe, e, 4)
                        for q in range(NQ):
                            ycp.wait(pe, e, q + 1 - 2)
                            for j in range(widths[q] // P):
                                ins = product(
                                    ps[:, 6 + q % 2, j * H:(j + 1) * H],
                                    lambda a, k: HS[:, a, k, (2 * q + j) * P:(2 * q + j + 1) * P],
                                    lambda b, k: WS[:, r, b, 4 + k, :],
                                )
                            ins.then_inc(yd.sem, 1)

                    turn(0, 0)
                    loop(pe, body)


        class Combine:

            def __init__(self, stack, tag, ring, more):
                self.ring = ring
                self.idx = sb([P, TB], U32, stack, "idx")
                self.gb = sb([P, TB], F32, stack, "gb")
                self.s1 = sb([P, TB], F32, stack, "s1")
                self.s2 = sb([P, TB], F32, stack, "s2")
                self.yg = sb([P, ring, CH, H], F32, stack, "yg")
                self.yg_in = [sem(f"{tag}_yg_in{r}") for r in range(ring)]
                self.ready = count(f"{tag}_idx_ready", 1)
                self.comb = count(f"{tag}_combined", NC, ring)
                self.ch = Chain(sem(f"{tag}_combine"), 1 + NC * 2 + more)

            def dve_begin(self, dve, a):
                self.ch.begin(a)
                b = bass.ds(TB * a, TB)
                dve.tensor_copy(self.idx[:], SLOT[:, b])
                dve.tensor_copy(self.gb[:], GATE[:, b])
                dve.tensor_scalar(self.s2[:], NMR[:, b], 0.5, None, ALU.mult)
                self.ch.link(dve, dve.tensor_scalar(self.s1[:], RSTD[:, b], 0.5, 1.0, ALU.mult, ALU.add))
                dve.sem_inc(self.ready.sem, 1)

            def pool_gather(self, pool, a, k):
                self.ready.wait(pool, a, 1)
                self.comb.wait_apart(pool, a, k + 1 - self.ring)
                for j in range(CH):
                    nc.gpsimd.indirect_dma_start(
                        out=self.yg[:, k % self.ring, j, :], out_offset=None, in_=y_rows,
                        in_offset=bass.IndirectOffsetOnAxis(ap=self.idx[:, CH * k + j:CH * k + j + 1], axis=0),
                    ).then_inc(self.yg_in[k % self.ring], 16)

            def dve(self, dve, a, k):
                for j in range(CH):
                    c = CH * k + j
                    x_t = X[:, TB * a + c, :]
                    ins = dve.tensor_scalar(x_t, x_t, self.s1[:, c:c + 1], self.s2[:, c:c + 1], ALU.mult, ALU.add)
                self.ch.link(dve, ins)
                dve.wait_ge(self.yg_in[k % self.ring],
                            a * (16 * CH * NC // self.ring) + 16 * CH * (k // self.ring + 1))
                for j in range(CH):
                    c = CH * k + j
                    x_t = X[:, TB * a + c, :]
                    ins = dve.scalar_tensor_tensor(x_t, self.yg[:, k % self.ring, j, :], self.gb[:, c:c + 1], x_t,
                                                   ALU.mult, ALU.add)
                self.ch.link(dve, ins)
                dve.sem_inc(self.comb.sem, 1)

        def attention():
            with ExitStack() as st:
                BG, BX, BZ, BY = 0, 1, 2, 3
                tail = Tail(st, "p3", (4, 5, 6, 7), 1, 2)
                comb = Combine(st, "p3", 2, NC + 3)
                s = lambda shape, dt=F32, name="a": sb(shape, dt, st, name)
                WA = s([P, 8, H], F32R)
                WC, WCT = s([P, HC, H]), s([P, HC, H])
                VEC = s([P, 6, HC])
                A1, B1, BD, NBD, ABD = (VEC[:, k, :] for k in range(5))
                RA, NA, RB, NB = s([P, TB]), s([P, TB]), s([P, TB]), s([P, TB])
                BSA, MVA, MRA, VEA = s([P, 2, CH, 6]), s([P, 2, CH, 2]), s([P, CH]), s([P, CH])
                XA = s([P, 2, CH, H + 1])
                XB = s([P, 2, CH, H])
                XS = s([P, 2, 2, HC, CT], F32R)
                AB = s([P, 2, HC, CT])
                CC = s([P, 2, HC, CT])
                YT = s([P, 2, HC, CT])
                TMP = s([P, HC, CT])
                NG = H + 1 + P + 1
                GS = s([P, NG])
                UV = s([P, 5, HC])
                s_w, s_set = sem("p3_w_in"), sem("p3_setup")
                stats = count("a_stats", NC)
                rstd = count("a_rstd", NC, 2)
                normed = count("a_normed", NC, 1)
                gd = count("a_gram", NC, 2)
                gs = count("a_gram_read", 1, 1)
                ucd = count("a_sums", 1)
                xbd = count("b_norm", NC)
                tb = count("b_turned", NC, 2)
                hi = count("b_hi", NC)
                lo = count("b_lo", NC, 1)
                zd = count("b_z", NC)
                lnd = count("b_log", NC)
                dz = count("b_softplus", NC, 1)
                scn = count("b_scan", NC, 2)
                e2d = count("b_da", NC, 2)
                yd = count("b_y", NC)
                yr = count("b_residual", NC, 2)
                x2 = count("b_x", NC, 1)
                ach = Chain(sem("a_pool"), 3 * NC)
                bch = Chain(sem("b_dve"), 1 + NC)
                cch = Chain(sem("b_act"), 2 * NC)
                block = st.enter_context(nc.Block())
                MID = BATCH - 2

                def turns(eng, body, last):
                    body(0, 1, None)
                    with eng.Fori(0, MID) as i:
                        body(i + 1, i + 2, i)
                    body(BATCH - 1, None, BATCH - 2)
                    last()

                @block.sync
                def _(sp):
                    tail.sp_setup()
                    sp.dma_start(WA[:].bitcast(F32).rearrange("p a b -> p (a b)"), w_ready).then_inc(s_w, 16)
                    for dst, src in ((WC, w_c), (WCT, w_c_t)):
                        sp.dma_start(dst[:], src.rearrange("(a p) e -> p a e", p=P)).then_inc(s_w, 16)
                    for k, v in enumerate((a_vec, b_vec, b_delta)):
                        sp.dma_start(VEC[:, k, :], v).then_inc(s_w, 16)
                    with sp.Fori(0, BATCH) as t:
                        for c in range(NC):
                            tail.sp_store(sp, t, c)

                @block.gpsimd
                def _(pool):
                    tail.pool_setup()
                    rstd.grant(pool)

                    def a_rstd(a, k):
                        if k == 0:
                            ach.begin(a)
                            normed.wait(pool, a, 0)
                        stats.wait_apart(pool, a, k + 1)
                        c = slice(CH * k, CH * k + CH)
                        mean, var = MVA[:, k % 2, :, 0], MVA[:, k % 2, :, 1]
                        ach.link(pool, nc.gpsimd.tensor_scalar(VEA[:], var, EPS, None, ALU.add))
                        ach.link(pool, nc.gpsimd.tensor_tensor(RA[:, c], VEA[:], NHALF, ALU.pow))
                        ach.link(pool, nc.gpsimd.tensor_tensor(MRA[:], mean, RA[:, c], ALU.mult), alone=True)
                        nc.gpsimd.tensor_scalar(NA[:, c], MRA[:], -1.0, None, ALU.mult).then_inc(rstd.sem, 1)

                    def body(t, a, p):
                        for s in range(NC + 3):
                            if 2 <= s < NC + 2:
                                tail.pool_rstd(pool, t, s - 2)
                            if a is not None and s >= 3:
                                a_rstd(a, s - 3)
                            if a is not None and 1 <= s <= NC:
                                comb.pool_gather(pool, a, s - 1)

                    for k in range(2):
                        comb.pool_gather(pool, 0, k)
                    for k in range(NC):
                        a_rstd(0, k)
                        if k + 2 < NC:
                            comb.pool_gather(pool, 0, k + 2)
                    turns(pool, body, lambda: None)

                @block.scalar
                def _(act):
                    tail.act_setup(act)
                    normed.grant(act)
                    e2d.grant(act)
                    act.wait_ge(s_w, 96)
                    act.wait_ge(s_set, 2)

                    def a_norm(a, k):
                        gd.wait(act, a, k - 1)
                        rstd.wait_apart(act, a, k + 1)
                        for j in range(CH):
                            c = CH * k + j
                            ins = act.activation(XA[:, k % 2, j, 0:H], X[:, TB * a + c, :], ACT.Identity,
                                                 bias=NA[:, c:c + 1], scale=RA[:, c:c + 1])
                        ins.then_inc(normed.sem, 1)

                    def x_hi(t, s):
                        tb.wait(act, t, s + 1)
                        yr.wait(act, t, s - 1)
                        act.copy(XS[:, s % 2, 0].rearrange("p a b -> p (a b)"), ps[:, BX, :]).then_inc(hi.sem, 1)

                    def softplus(t, s):
                        if s == 0:
                            cch.begin(t)
                        zd.wait(act, t, s + 1)
                        scn.wait(act, t, s - 1)
                        e2d.wait(act, t, s - 1)
                        for h in range(HC):
                            ins = act.activation(AB[:, s % 2, h, :], ps[:, BZ, h * CT:(h + 1) * CT], ACT.Abs,
                                                 bias=BD[:, h:h + 1])
                        cch.link(act, ins)
                        cch.link(act, act.activation(AB[:, s % 2], AB[:, s % 2], ACT.Exp, scale=-1.0))
                        act.activation(AB[:, s % 2], AB[:, s % 2], ACT.Ln, bias=1.0).then_inc(lnd.sem, 1)

                    def d_a(t, s):
                        dz.wait(act, t, s + 1)
                        yr.wait(act, t, s - 1)
                        for h in range(HC):
                            ins = act.activation(YT[:, s % 2, h, :], AB[:, s % 2, h, :], ACT.Exp,
                                                 bias=ABD[:, h:h + 1], scale=A1[:, h:h + 1])
                        ins.then_inc(e2d.sem, 1)

                    def body(t, a, p):
                        for s in range(NC + 3):
                            if s < NC:
                                x_hi(t, s)
                            if 1 <= s <= NC:
                                d_a(t, s - 1)
                            if s == 1 and p is not None:
                                tail.act_exp(act, p)
                            if 2 <= s < NC + 2:
                                tail.act_norm(act, t, s - 2)
                            if a is not None and s >= 3:
                                a_norm(a, s - 3)
                            if s < NC:
                                softplus(t, s)
                            if 2 <= s < NC + 2:
                                tail.act_evac(act, t, s - 2)

                    for k in range(NC):
                        a_norm(0, k)
                    turns(act, body, lambda: tail.act_exp(act, BATCH - 1))

                @block.vector
                def _(dve):
                    for c in (gs, lo, dz, scn, x2, comb.comb):
                        c.grant(dve)
                    tail.dve_setup()
                    dve.memset(XA[:, :, :, H:H + 1], 1.0)
                    dve.wait_ge(s_w, 96)
                    dve.tensor_scalar(NBD, BD, -1.0, None, ALU.mult).then_inc(s_set, 1)
                    dve.tensor_tensor(ABD, A1, BD, ALU.mult).then_inc(s_set, 1)
                    dve.wait_ge(s_set, 2)

                    def a_chunk(a, k):
                        comb.dve(dve, a, k)
                        rstd.wait_apart(dve, a, k - 1)
                        for j in range(CH):
                            ins = dve.bn_stats(BSA[:, k % 2, j, :], X[:, TB * a + (CH * k + j), :])
                        comb.ch.link(dve, ins, alone=True)
                        for j in range(CH):
                            ins = dve.bn_aggr(MVA[:, k % 2, j, :], BSA[:, k % 2, j, :])
                        ins.then_inc(stats.sem, 1)

                    def a_sums(a):
                        gd.wait(dve, a, NC)
                        dve.tensor_copy(GS[:], ps[:, BG, 0:NG]).then_inc(gs.sem, 1)
                        ucd.wait(dve, a, 1)
                        sums = ps[:, tail.bc, :]
                        scratch = TMP[:].rearrange("p a b -> p (a b)")
                        for n, (l, r) in enumerate(((WC[:, 0, :], GS[:, 0:H]), (WC[:, 1, 0:P], sums[:, 0:P]),
                                                    (WC[:, 1, P:H], GS[:, H + 1:H + 1 + P]))):
                            o = (0, H, H + P)[n]
                            ins = dve.tensor_tensor_reduce(out=scratch[:, o:o + l.shape[1]], in0=l, in1=r, scale=1.0,
                                                           scalar=0.0, op0=ALU.mult, op1=ALU.add,
                                                           accum_out=UV[:, 2 + n // 2, n % 2:n % 2 + 1])
                        comb.ch.link(dve, ins)
                        comb.ch.link(dve, dve.tensor_tensor(UV[:, 2, 1:2], UV[:, 2, 1:2], UV[:, 3, 0:1], ALU.add))
                        dve.tensor_tensor(UV[:, 0, :], UV[:, 2, :], B1, ALU.mult)
                        comb.ch.link(dve, dve.tensor_tensor(UV[:, 1, :], sums[:, P:P + HC], B1, ALU.mult))
                        comb.ch.end()

                    def b_norm(t, s):
                        tb.wait(dve, t, s - 1)
                        for j in range(CH):
                            c = CH * s + j
                            ins = dve.tensor_scalar(XB[:, s % 2, j, :], X[:, TB * t + c, :], RB[:, c:c + 1],
                                                    NB[:, c:c + 1], ALU.mult, ALU.add)
                        ins.then_inc(xbd.sem, 1)

                    def x_lo(t, s):
                        hi.wait(dve, t, s + 1)
                        dve.tensor_tensor(XS[:, s % 2, 1].rearrange("p a b -> p (a b)"), ps[:, BX, :],
                                          XS[:, s % 2, 0].bitcast(F32).rearrange("p a b -> p (a b)"),
                                          ALU.subtract).then_inc(lo.sem, 1)

                    def y(t, s):
                        e2d.wait(dve, t, s + 1)
                        scn.wait(dve, t, s + 1)
                        for h in range(HC):
                            ins = dve.tensor_scalar(TMP[:, h, :], CC[:, s % 2, h, :], UV[:, 1, h:h + 1], None, ALU.mult)
                        bch.link(dve, ins)
                        for h in range(HC):
                            ins = dve.scalar_tensor_tensor(YT[:, s % 2, h, :], YT[:, s % 2, h, :], UV[:, 0, h:h + 1],
                                                           TMP[:, h, :], ALU.mult, ALU.add)
                        ins.then_inc(yd.sem, 1)

                    def scan(t, s):
                        lnd.wait(dve, t, s + 1)
                        for h in range(HC):
                            ins = dve.scalar_tensor_tensor(AB[:, s % 2, h, :], ps[:, BZ, h * CT:(h + 1) * CT],
                                                           NBD[:, h:h + 1], AB[:, s % 2, h, :], ALU.max, ALU.add)
                        ins.then_inc(dz.sem, 1)
                        dz.wait(dve, t, s + 1)
                        scn.wait(dve, t, s)
                        for h in range(HC):
                            start = 0.0 if s == 0 else CC[:, 1 - s % 2, h, CT - 1:CT]
                            ins = dve.tensor_tensor_scan(CC[:, s % 2, h, :], BD[:, h:h + 1].to_broadcast([P, CT]),
                                                         AB[:, s % 2, h, :], start, ALU.add, ALU.add)
                        ins.then_inc(scn.sem, 1)

                    def x_new(t, s):
                        yr.wait(dve, t, s + 1)
                        x_t = X[:, bass.ds(TB * t + CH * s, CH), :].rearrange("p a b -> p (a b)")
                        dve.tensor_tensor(x_t, x_t, ps[:, BY, :], ALU.add).then_inc(x2.sem, 1)
                        x2.wait(dve, t, s + 1)

                    def body(t, a, p):
                        bch.begin(t)
                        rstd.wait(dve, t, NC)
                        dve.tensor_copy(RB[:], RA[:])
                        bch.link(dve, dve.tensor_copy(NB[:], NA[:]))
                        b_norm(t, 0)
                        if a is not None:
                            comb.dve_begin(dve, a)
                        for s in range(NC + 3):
                            if 2 <= s < NC + 2:
                                x_new(t, s - 2)
                                tail.dve_stats(dve, t, s - 2)
                            if s < NC:
                                x_lo(t, s)
                            if s < NC - 1:
                                b_norm(t, s + 1)
                            if a is not None and s >= 3:
                                a_chunk(a, s - 3)
                            if 1 <= s <= NC:
                                y(t, s - 1)
                            if s < NC:
                                scan(t, s)
                            if p is not None and s < 7:
                                tail.post(dve, p, s)
                        tail.dve_keep(dve, t)
                        bch.end()
                        if a is not None:
                            a_sums(a)

                    comb.dve_begin(dve, 0)
                    for k in range(NC):
                        a_chunk(0, k)
                    a_sums(0)

                    def rest():
                        for k in range(7):
                            tail.post(dve, BATCH - 1, k)
                        tail.dve_finish(dve)

                    turns(dve, body, rest)

                @block.tensor
                def _(pe):
                    tail.pe_setup(pe)
                    for c in (gd, tb, yr):
                        c.grant(pe)
                    pe.wait_ge(s_w, 96)

                    def gram(a, k):
                        normed.wait(pe, a, k + 1)
                        if k == 0:
                            gs.wait(pe, a, 0)
                        for j in range(CH):
                            x_c = XA[:, k % 2, j, :]
                            first = k == 0 and j == 0
                            end = k == NC - 1 and j == CH - 1
                            pe.matmul(ps[:, BG, 0:H + 1], x_c[:, 0:P], x_c, start=first, stop=end,
                                      skip_group_check=True)
                            ins = pe.matmul(ps[:, BG, H + 1:NG], x_c[:, P:H], x_c[:, P:H + 1], start=False, stop=end,
                                            skip_group_check=True)
                        ins.then_inc(gd.sem, 1)

                    def sums(a):
                        gs.wait(pe, a, 1)
                        pe.transpose(ps[:, tail.bc, 0:P], GS[:, P:H], IDENT)
                        for h in range(HC):
                            for k in range(HC):
                                ins = pe.matmul(ps[:, tail.bc, P + h:P + h + 1], WCT[:, k, h * P:(h + 1) * P],
                                                GS[:, (H, NG - 1)[k]:(H, NG - 1)[k] + 1], start=(k == 0),
                                                stop=(k == HC - 1))
                        ins.then_inc(ucd.sem, 1)

                    def turn(t, s):
                        xbd.wait(pe, t, s + 1)
                        lo.wait(pe, t, s)
                        for h in range(HC):
                            for j in range(CH):
                                o = h * CT + j * P
                                ins = pe.transpose(ps[:, BX, o:o + P], XB[:, s % 2, j, h * P:(h + 1) * P], IDENT)
                        ins.then_inc(tb.sem, 1)

                    terms = [(a, b, k) for k in range(HC) for a, b in ((0, 0), (0, 1), (1, 0))]

                    def delta(t, s):
                        lo.wait(pe, t, s + 1)
                        dz.wait(pe, t, s)
                        for h in range(HC):
                            for n, (a, b, k) in enumerate(terms):
                                ins = pe.matmul(ps[:, BZ, h * CT:(h + 1) * CT], WA[:, 2 * a + k, h * P:(h + 1) * P],
                                                XS[:, s % 2, b, k, :], start=(n == 0), stop=(n == len(terms) - 1))
                        ins.then_inc(zd.sem, 1)

                    def residual(t, s):
                        yd.wait(pe, t, s + 1)
                        x2.wait(pe, t, s)
                        for j in range(CH):
                            for n, (a, b, k) in enumerate(terms):
                                pe.matmul(ps[:, BY, j * H:(j + 1) * H], XS[:, s % 2, a, k, j * P:(j + 1) * P],
                                          WA[:, 4 + 2 * b + k, :], start=(n == 0), stop=False, skip_group_check=True)
                            for h in range(HC):
                                ins = pe.matmul(ps[:, BY, j * H + h * P:j * H + (h + 1) * P],
                                                YT[:, s % 2, h, j * P:(j + 1) * P], IDENT, is_transpose=True,
                                                start=False, stop=(h == HC - 1), skip_group_check=True)
                        ins.then_inc(yr.sem, 1)

                    def body(t, a, p):
                        for s in range(NC + 4):
                            if s < NC:
                                turn(t, s)
                            if 3 <= s < NC + 3:
                                tail.pe_logits(pe, t, s - 3)
                            if a is not None and s >= 4:
                                gram(a, s - 4)
                            if s < NC:
                                delta(t, s)
                            if p is not None and s == 1:
                                tail.pe_count(pe, p)
                            if p is not None and 4 <= s < 8:
                                tail.pe_inv(pe, p, s - 4)
                            if 2 <= s < NC + 2:
                                tail.pe_turn(pe, t, s - 2)
                            if 1 <= s <= NC:
                                residual(t, s - 1)
                        if a is not None:
                            sums(a)

                    for k in range(NC):
                        gram(0, k)
                    sums(0)

                    def rest():
                        tail.pe_count(pe, BATCH - 1)
                        for q in range(4):
                            tail.pe_inv(pe, BATCH - 1, q)
                        tail.pe_finish(pe)

                    turns(pe, body, rest)

        def finish():
            with ExitStack() as st:
                comb = Combine(st, "p5", 8, 0)
                s_out = sem("out_stored")
                block = st.enter_context(nc.Block())
                rows = out.rearrange("(b k j p) d -> b k p j d", p=P, j=CH, k=NC)

                @block.sync
                def _(sp):
                    with sp.Fori(0, BATCH) as a:
                        for k in range(NC):
                            comb.comb.wait(sp, a, k + 1)
                            sp.dma_start(rows[a, k], X[:, bass.ds(TB * a + CH * k, CH), :]).then_inc(s_out, 16)
                    sp.wait_ge(s_out, 16 * BATCH * NC)

                @block.gpsimd
                def _(pool):
                    with pool.Fori(0, BATCH) as a:
                        for k in range(NC):
                            comb.pool_gather(pool, a, k)

                @block.vector
                def _(dve):
                    comb.comb.grant(dve)
                    with dve.Fori(0, BATCH) as a:
                        comb.dve_begin(dve, a)
                        for k in range(NC):
                            comb.dve(dve, a, k)
                        comb.ch.end()

        experts("p2")
        attention()
        experts("p4")
        finish()


_ARRAYS = ["x", "w_proj0", "w_delta_t", "w_c", "w_c_t", "w_r_t", "a_vec", "b_vec", "d_vec", "b_delta",
           "w_router", "w_gate", "w_up", "w_down", "c_f32", "c_bf16"]


def kernel(L0_attn_x, L0_attn_W_proj, L0_attn_A, L0_attn_Bp, L0_attn_D, L0_attn_W_delta, L0_attn_b_delta,
           L0_ffn_w_router, L0_ffn_w_gate, L0_ffn_w_up, L0_ffn_w_down):
    import concourse.bacc as bacc
    import ml_dtypes
    import numpy as np
    from concourse.bass_utils import run_bass_kernel_spmd

    def c(a):
        return np.ascontiguousarray(a)

    def halves(v):
        return c(np.asarray(v).reshape(HC, P).T)

    w = np.asarray(L0_attn_W_proj)
    i, f = np.arange(P), np.float32
    c_f32 = np.concatenate([np.eye(P, dtype=f), np.tile((E - np.arange(E)).astype(f), (P, 1)),
                            i[:, None].astype(f), np.tile(np.arange(TB).astype(f), (P, 1)),
                            np.full((P, CH), -0.5, f)], axis=1)
    c_bf16 = np.concatenate([(i[:, None] <= i[None, :]).astype(f), np.ones((P, P), f), np.tile(i.astype(f), (P, 1)),
                             np.tile(np.arange(ST).astype(f), (P, 1)), np.zeros((P, P), f)],
                            axis=1).astype(ml_dtypes.bfloat16)
    arrays = dict(
        x=c(np.asarray(L0_attn_x).reshape(T, H)), w_proj0=c(w[0:H]), w_delta_t=c(np.asarray(L0_attn_W_delta).T),
        w_c=c(w[2 * H:3 * H]), w_c_t=c(w[2 * H:3 * H].T), w_r_t=c(w[3 * H:4 * H].T), a_vec=halves(L0_attn_A),
        b_vec=halves(L0_attn_Bp), d_vec=c(np.broadcast_to(np.asarray(L0_attn_D).reshape(1, 1), (P, 1))),
        b_delta=halves(L0_attn_b_delta), w_router=c(L0_ffn_w_router), w_gate=c(L0_ffn_w_gate),
        w_up=c(L0_ffn_w_up), w_down=c(L0_ffn_w_down), c_f32=c_f32, c_bf16=c_bf16)
    nc = bacc.Bacc("TRN2", target_bir_lowering=False, num_devices=1)
    feeds, args = {}, []
    for name in _ARRAYS:
        a = arrays[name]
        feeds[f"in_{name}"] = a
        args.append(nc.dram_tensor(f"in_{name}", a.shape, mybir.dt.from_np(a.dtype), kind="ExternalInput").ap())
    out = nc.dram_tensor("out", [T, H], F32, kind="ExternalOutput").ap()
    macaron(nc, *args, out)
    r = run_bass_kernel_spmd(nc, [feeds], core_ids=[0])
    return r.results[0]["out"].reshape(BATCH, SEQ, H)
```

```python
from contextlib import ExitStack

import concourse.bass as bass
from concourse import mybir

ALU = mybir.AluOpType
ACT = mybir.ActivationFunctionType
AX = mybir.AxisListType.X
F32 = mybir.dt.float32
F32R = mybir.dt.float32r
BF16 = mybir.dt.bfloat16
U32 = mybir.dt.uint32

P = 128
H = 256
HC = H // P
E = 32
F = 256
BATCH, SEQ = 8, 2048
T = BATCH * SEQ
NT = T // P
TB = SEQ // P
CAP = -(-5 * T // (4 * E))
ET = CAP // P
ST = E * ET
DROP = E * CAP
CH = 2
NC = TB // CH
CT = CH * P
EPS = 1e-5
SL = CAP // 2
assert CAP % P == 0 and SL >= 256 and SL <= 512


PASSED = {}


def apart(eng):
    eng.sem_inc(PASSED[eng.engine], 1)


class Count:

    def __init__(self, sem, per, credit=0):
        self.sem, self.per, self.credit = sem, per, credit

    def wait(self, eng, turn, n):
        assert n + self.credit >= 1
        eng.wait_ge(self.sem, turn * self.per + (n + self.credit))

    def wait_apart(self, eng, turn, n):
        self.wait(eng, turn, n)
        apart(eng)

    def grant(self, eng):
        eng.sem_inc(self.sem, self.credit)


class Chain:

    def __init__(self, sem, per):
        self.sem, self.per = sem, per
        self.turn, self.n = 0, 0

    def begin(self, turn):
        self.turn, self.n = turn, 0

    def link(self, eng, ins, alone=False):
        self.n += 1
        ins.then_inc(self.sem, 1)
        eng.wait_ge(self.sem, self.turn * self.per + self.n)
        if alone:
            apart(eng)

    def end(self):
        assert self.n == self.per, (self.n, self.per)


def macaron(nc, x, w_proj0, w_delta_t, w_c, w_c_t, w_r_t, a_vec, b_vec, d_vec, b_delta,
            w_router, w_gate, w_up, w_down, c_f32, c_bf16, out):
    with ExitStack() as ctx:
        names = [0]

        def sb(shape, dt=F32, stack=ctx, name="t"):
            names[0] += 1
            return stack.enter_context(nc.sbuf_tensor(f"{name}_{names[0]}", shape, dt))

        def sem(name):
            names[0] += 1
            return ctx.enter_context(nc.semaphore(f"{name}_{names[0]}"))

        def count(name, per, credit=0):
            return Count(sem(name), per, credit)

        for eng in (nc.vector, nc.scalar, nc.gpsimd):
            PASSED[eng.engine] = sem("passed")

        xn_rows = nc.dram_tensor("xn_rows", [T, H], F32, kind="Internal").ap()
        y_rows = nc.dram_tensor("y_rows", [DROP + P, H], F32, kind="Internal").ap()
        w_ready = nc.dram_tensor("w_ready", [P, 8 * H], F32, kind="Internal").ap()

        ps = ctx.enter_context(nc.psum_tensor("ps", [P, 8, 512], F32))

        X = sb([P, NT, H], name="x")
        RSTD = sb([P, NT], name="rstd")
        NMR = sb([P, NT], name="nmr")
        GATE = sb([P, NT], name="gate")
        SLOT = sb([P, NT], U32, name="slot")
        INV = sb([P, ST], U32, name="inv")
        CF = sb([P, 128 + 32 + 1 + 16 + CH], F32, name="cf")
        CB = sb([P, 128 * 3 + 160 + 128], BF16, name="cb")
        WR = sb([P, HC, E], F32, name="wr")
        IDENT = CF[:, 0:128]
        REV = CF[:, 128:160]
        LANE = CF[:, 160:161]
        IOTA16 = CF[:, 161:177]
        NHALF = CF[:, 177:177 + CH]
        TRI = CB[:, 0:128]
        ONES = CB[:, 128:256]
        IOTA128 = CB[:, 256:384]
        IOTA160 = CB[:, 384:544]
        BZERO = CB[:, 544:672]
        sbuf_base = [0]

        def mid(ap, n):
            return ap.unsqueeze(1).to_broadcast([P, n, ap.shape[1]])

        def last(ap, k):
            return ap.unsqueeze(2).to_broadcast([P, ap.shape[1], k])

        class Tail:

            def __init__(self, stack, tag, banks, n_t, xr):
                self.bt, self.bl, self.bc, self.bi = banks
                self.n_t, self.xr = n_t, xr
                s = lambda shape, dt=F32, name="r": sb(shape, dt, stack, name)
                self.bs = s([P, 2, CH, 6])
                self.mv = s([P, 2, CH, 2])
                self.rb = s([P, TB])
                self.nb = s([P, TB])
                self.mr = s([P, CH])
                self.ve = s([P, CH])
                self.xn = s([P, xr, CH, H])
                self.xt = s([P, 2, HC, CH, P])
                self.d = s([P, TB, E])
                self.cand = s([P, TB, E])
                self.oh = s([P, TB, E], BF16)
                self.small = s([P, 12, TB])
                self.slu = s([P, 3, TB], U32)
                self.carry = s([P, E], BF16)
                self.cr = s([P, E])
                self.oa = s([P, 2, 4, P], BF16)
                self.ob = s([P, 2, 4, 2, ST], BF16)
                self.inv_f = self.d[:].rearrange("p t e -> p (t e)")[:, 0:ST]
                self.inv_g = self.cand[:].rearrange("p t e -> p (t e)")[:, 0:ST]
                self.stats = count(f"{tag}_stats", NC)
                self.rdone = count(f"{tag}_rstd", NC, 2)
                self.kept = count(f"{tag}_kept", 1, 1)
                self.normed = count(f"{tag}_normed", NC, 1)
                self.st = [sem(f"{tag}_rows_stored{k}") for k in range(xr)]
                self.free = count(f"{tag}_rows_free", NC, xr)
                self.turned = count(f"{tag}_turned", NC, xr)
                self.evac = count(f"{tag}_evac", NC, n_t)
                self.logits = count(f"{tag}_logits", NC, 2)
                self.lread = count(f"{tag}_logits_read", 1, 1)
                self.expd = count(f"{tag}_exp", 1)
                self.ohd = count(f"{tag}_onehot", 1)
                self.cnt = count(f"{tag}_count", 1)
                self.hot = count(f"{tag}_hot", 4)
                self.inv = count(f"{tag}_inv", 4, 2)
                self.fin = sem(f"{tag}_inv_fin")
                self.dch = Chain(sem(f"{tag}_dve"), NC)
                self.pch = Chain(sem(f"{tag}_pool"), 3 * NC)
                self.post_ch = Chain(sem(f"{tag}_post"), 18)
                self.setup_done = sem(f"{tag}_setup")

            def dve_setup(self):
                nc.vector.memset(self.carry[:], 0.0)
                nc.vector.tensor_scalar(self.small[:, 11, :], IOTA16, float(-TB), None,
                                        ALU.add).then_inc(self.setup_done, 1)
                nc.vector.wait_ge(self.setup_done, 1)
                self.lread.grant(nc.vector)
                self.kept.grant(nc.vector)

            def dve_stats(self, dve, t, c):
                if c == 0:
                    self.dch.begin(t)
                self.rdone.wait_apart(dve, t, c - 1)
                for j in range(CH):
                    ins = dve.bn_stats(self.bs[:, c % 2, j, :], X[:, TB * t + (CH * c + j), :])
                self.dch.link(dve, ins, alone=True)
                for j in range(CH):
                    ins = dve.bn_aggr(self.mv[:, c % 2, j, :], self.bs[:, c % 2, j, :])
                ins.then_inc(self.stats.sem, 1)

            def dve_keep(self, dve, t):
                self.rdone.wait_apart(dve, t, NC)
                dve.tensor_copy(RSTD[:, bass.ds(TB * t, TB)], self.rb[:])
                dve.tensor_copy(NMR[:, bass.ds(TB * t, TB)], self.nb[:]).then_inc(self.kept.sem, 1)
                self.dch.end()

            def pool_setup(self):
                self.rdone.grant(nc.gpsimd)

            def pool_rstd(self, pool, t, c):
                if c == 0:
                    self.pch.begin(t)
                    self.kept.wait(pool, t, 0)
                    self.normed.wait(pool, t, 0)
                self.stats.wait_apart(pool, t, c + 1)
                rb = self.rb[:, CH * c:CH * c + CH]
                nb = self.nb[:, CH * c:CH * c + CH]
                mean, var = self.mv[:, c % 2, :, 0], self.mv[:, c % 2, :, 1]
                self.pch.link(pool, nc.gpsimd.tensor_scalar(self.ve[:], var, EPS, None, ALU.add))
                self.pch.link(pool, nc.gpsimd.tensor_tensor(rb, self.ve[:], NHALF, ALU.pow))
                self.pch.link(pool, nc.gpsimd.tensor_tensor(self.mr[:], mean, rb, ALU.mult), alone=True)
                nc.gpsimd.tensor_scalar(nb, self.mr[:], -1.0, None, ALU.mult).then_inc(self.rdone.sem, 1)
                if c == NC - 1:
                    self.pch.end()

            def act_setup(self, act):
                self.evac.grant(act)
                self.normed.grant(act)

            def act_norm(self, act, t, c):
                self.free.wait(act, t, c + 1 - self.xr)
                self.turned.wait(act, t, c + 1 - self.xr)
                self.rdone.wait_apart(act, t, c + 1)
                for j in range(CH):
                    k = CH * c + j
                    ins = act.activation(self.xn[:, c % self.xr, j, :], X[:, TB * t + k, :], ACT.Identity,
                                         bias=self.nb[:, k:k + 1], scale=self.rb[:, k:k + 1])
                ins.then_inc(self.normed.sem, 1)

            def act_evac(self, act, t, c):
                self.turned.wait(act, t, c + 1)
                self.logits.wait(act, t, c - 1)
                act.copy(self.xt[:, c % 2].rearrange("p a b c -> p (a b c)"),
                         ps[:, self.bt + c % self.n_t, :]).then_inc(self.evac.sem, 1)

            def act_exp(self, act, p):
                self.post_ch_wait(act, p, 3)
                act.activation(self.d[:], self.d[:], ACT.Exp).then_inc(self.expd.sem, 1)

            def post_ch_wait(self, eng, p, n):
                eng.wait_ge(self.post_ch.sem, p * self.post_ch.per + n)

            def sp_setup(self):
                self.free.grant(nc.sync)

            def sp_free(self, sp, t, c):
                sp.wait_ge(self.st[c % self.xr], t * (16 * NC // self.xr) + 16 * (c // self.xr + 1))
                sp.sem_inc(self.free.sem, 1)

            def sp_store(self, sp, t, c):
                self.normed.wait(sp, t, c + 1)
                rows = xn_rows.rearrange("(k j p) d -> k p j d", p=P, j=CH)
                sp.dma_start(rows[t * NC + c], self.xn[:, c % self.xr]).then_inc(self.st[c % self.xr], 16)
                lag = self.xr // 2
                if c >= lag:
                    self.sp_free(sp, t, c - lag)
                if c == NC - 1:
                    for k in range(NC - lag, NC):
                        self.sp_free(sp, t, k)

            def pe_setup(self, pe):
                self.turned.grant(pe)
                self.evac_n = 0
                self.logits.grant(pe)
                self.inv.grant(pe)
                for k in range(2):
                    pe.matmul(ps[:, self.bi, ST * k:ST * k + ST], BZERO, IOTA160, start=(k == 0), stop=False,
                              skip_group_check=True)

            def pe_turn(self, pe, t, c):
                self.normed.wait(pe, t, c + 1)
                self.evac.wait(pe, t, c + 1 - self.n_t)
                for j in range(CH):
                    for h in range(HC):
                        o = (h * CH + j) * P
                        ins = pe.transpose(ps[:, self.bt + c % self.n_t, o:o + P],
                                           self.xn[:, c % self.xr, j, h * P:(h + 1) * P], IDENT)
                ins.then_inc(self.turned.sem, 1)

            def pe_logits(self, pe, t, c):
                self.evac.wait(pe, t, c + 1)
                if c == 0:
                    self.lread.wait(pe, t, 0)
                for j in range(CH):
                    k = CH * c + j
                    for h in range(HC):
                        ins = pe.matmul(ps[:, self.bl, k * E:(k + 1) * E], self.xt[:, c % 2, h, j, :],
                                        WR[:, h, :], start=(h == 0), stop=(h == HC - 1))
                ins.then_inc(self.logits.sem, 1)

            def post(self, dve, p, step):
                ch, s = self.post_ch, self.small
                lg = ps[:, self.bl, :].rearrange("p (t e) -> p t e", e=E)
                ct = ps[:, self.bc, :].rearrange("p (t e) -> p t e", e=E)
                mx, rr, se, gt, ci, acc, t1, t2, slf, lo, hi, tid = (s[:, k, :] for k in range(12))
                if step == 0:
                    ch.begin(p)
                    self.logits.wait(dve, p, NC)
                    ch.link(dve, dve.reduce_max(mx, lg, AX))
                    ch.link(dve, dve.tensor_tensor(self.d[:], lg, last(mx, E), ALU.subtract))
                    if self.bl != self.bc:
                        dve.sem_inc(self.lread.sem, 1)
                    ch.link(dve, dve.scalar_tensor_tensor(self.cand[:], self.d[:], 0.0, mid(REV, TB), ALU.is_ge,
                                                          ALU.mult))
                    ch.link(dve, dve.reduce_max(rr, self.cand[:], AX))
                    dve.tensor_tensor(self.oh[:], mid(REV, TB), last(rr, E), ALU.is_equal).then_inc(self.ohd.sem, 1)
                if step == 1:
                    self.expd.wait(dve, p, 1)
                    ch.link(dve, dve.reduce_sum(se, self.d[:], AX))
                    ch.link(dve, dve.reciprocal(gt, se))
                if step == 2:
                    self.cnt.wait(dve, p, 1)
                    ch.link(dve, dve.tensor_tensor(self.cand[:], self.oh[:], ct, ALU.mult))
                    if self.bl == self.bc:
                        dve.sem_inc(self.lread.sem, 1)
                    ch.link(dve, dve.reduce_sum(ci, self.cand[:], AX))
                    ch.link(dve, dve.reduce_sum(self.cr[:], self.oh[:].rearrange("p t e -> p e t"), AX))
                    ch.link(dve, dve.tensor_tensor(self.carry[:], self.carry[:], self.cr[:], ALU.add))
                    ch.link(dve, dve.tensor_scalar(acc, ci, float(CAP), None, ALU.is_le))
                    ch.link(dve, dve.scalar_tensor_tensor(t1, rr, float(-CAP), ci, ALU.mult, ALU.add))
                    ch.link(dve, dve.scalar_tensor_tensor(t2, t1, -1.0, acc, ALU.add, ALU.mult))
                    ch.link(dve, dve.tensor_scalar(slf, t2, float(DROP), None, ALU.add))
                    ch.link(dve, dve.tensor_copy(self.slu[:, 0, :], slf), alone=True)
                    dve.tensor_copy(SLOT[:, bass.ds(TB * p, TB)], self.slu[:, 0, :])
                    dve.tensor_scalar(self.slu[:, 1, :], self.slu[:, 0, :], P - 1, None, ALU.bitwise_and)
                    ch.link(dve, dve.tensor_scalar(self.slu[:, 2, :], self.slu[:, 0, :], 7, None,
                                                   ALU.logical_shift_right))
                    dve.tensor_copy(lo, self.slu[:, 1, :])
                    dve.tensor_copy(hi, self.slu[:, 2, :])
                    dve.tensor_scalar(tid, tid, float(TB), None, ALU.add)
                    ch.link(dve, dve.scalar_tensor_tensor(GATE[:, bass.ds(TB * p, TB)], gt, 0.5, acc,
                                                          ALU.mult, ALU.mult))
                if step >= 3:
                    q = step - 3
                    self.inv.wait(dve, p, q + 1 - 2)
                    for k in range(4):
                        j = 4 * q + k
                        dve.tensor_scalar(self.oa[:, q % 2, k, :], IOTA128, lo[:, j:j + 1], None, ALU.is_equal)
                        dve.tensor_scalar(self.ob[:, q % 2, k, 0, :], IOTA160, hi[:, j:j + 1], tid[:, j:j + 1],
                                          ALU.is_equal, ALU.mult)
                        ins = dve.tensor_scalar(self.ob[:, q % 2, k, 1, :], IOTA160, hi[:, j:j + 1], LANE,
                                                ALU.is_equal, ALU.mult)
                    ins.then_inc(self.hot.sem, 1)
                if step == 6:
                    self.hot.wait(dve, p, 4)
                    dve.sem_inc(ch.sem, 1)
                    ch.n += 1
                    ch.end()

            def pe_count(self, pe, p):
                self.ohd.wait(pe, p, 1)
                ct = ps[:, self.bc, :].rearrange("p (t e) -> p t e", e=E)
                pe.matmul(ct, ONES, mid(self.carry[:], TB), start=True, stop=False, skip_group_check=True)
                for j in range(TB - 1):
                    pe.matmul(ct[:, j + 1:, :], ONES, mid(self.oh[:, j, :], TB - 1 - j), start=False, stop=False,
                              skip_group_check=True)
                pe.matmul(ct, TRI, self.oh[:], start=False, stop=True,
                          skip_group_check=True).then_inc(self.cnt.sem, 1)

            def pe_inv(self, pe, p, q):
                self.hot.wait(pe, p, q + 1)
                for k in range(4):
                    ins = pe.matmul(ps[:, self.bi, 0:2 * ST], self.oa[:, q % 2, k, :], self.ob[:, q % 2, k],
                                    start=False, stop=False, skip_group_check=True)
                ins.then_inc(self.inv.sem, 1)

            def pe_finish(self, pe):
                for k in range(2):
                    ins = pe.matmul(ps[:, self.bi, ST * k:ST * k + ST], BZERO, IOTA160, start=False,
                                    stop=(k == 1), skip_group_check=True)
                ins.then_inc(self.fin, 1)

            def dve_finish(self, dve):
                dve.wait_ge(self.fin, 1)
                dve.tensor_copy(self.inv_f, ps[:, self.bi, ST:2 * ST]).then_inc(self.fin, 1)
                dve.wait_ge(self.fin, 2)
                dve.scalar_tensor_tensor(self.inv_g, ps[:, self.bi, 0:ST], float(P), self.inv_f,
                                         ALU.mult, ALU.add).then_inc(self.fin, 1)
                dve.wait_ge(self.fin, 3)
                dve.tensor_copy(INV[:], self.inv_g)

        with ExitStack() as st:
            tail = Tail(st, "p1", (0, 2, 3, 4), 2, 4)
            s_const = sem("const_in")
            s_x = [sem(f"x_in{g}") for g in range(4)]
            s_w = sem("w_in")
            s_prep, s_prepd, s_wout = sem("prep"), sem("prep_done"), sem("w_out")
            s_zero, s_zout = sem("zero"), sem("zero_out")
            WIN = sb([P, 6, H], F32, st, "win")
            WOUT = sb([P, 8, H], F32R, st, "wout")
            DV = sb([P, 1], F32, st, "dv")
            WT = sb([P, 2, H], F32, st, "wt")
            zero = sb([P, H], F32, st, "zero")
            block = st.enter_context(nc.Block())
            x_in = x.rearrange("(b g j p) d -> b g p j d", p=P, j=4, g=4)

            def load(sp, b, g):
                sp.dma_start(X[:, bass.ds(TB * b + 4 * g, 4), :], x_in[b, g]).then_inc(s_x[g], 16)

            @block.sync
            def _(sp):
                tail.sp_setup()
                sp.dma_start(CF[:], c_f32).then_inc(s_const, 16)
                sp.dma_start(CB[:], c_bf16).then_inc(s_const, 16)
                sp.dma_start(WR[:], w_router.rearrange("(a p) e -> p a e", p=P)).then_inc(s_const, 16)
                for g in range(4):
                    load(sp, 0, g)
                for k, w in enumerate((w_proj0, w_delta_t, w_r_t)):
                    sp.dma_start(WIN[:, 2 * k:2 * k + 2, :], w.rearrange("(a p) e -> p a e", p=P)).then_inc(s_w, 16)
                sp.dma_start(DV[:], d_vec.to_broadcast([P, 1])).then_inc(s_w, 16)
                sp.wait_ge(s_zero, 1)
                sp.dma_start(y_rows[DROP:DROP + P, :], zero[:]).then_inc(s_zout, 16)

                def turn(t, more):
                    for c in range(NC):
                        if more and c % 2 == 0:
                            tail.stats.wait(sp, t, c + 2)
                            load(sp, t + 1, c // 2)
                        tail.sp_store(sp, t, c)

                with sp.Fori(0, BATCH - 1) as b:
                    turn(b, True)
                turn(BATCH - 1, False)
                sp.wait_ge(s_prepd, 5)
                sp.dma_start(w_ready, WOUT[:].bitcast(F32).rearrange("p a b -> p (a b)")).then_inc(s_wout, 16)
                sp.wait_ge(s_wout, 16)
                sp.wait_ge(s_zout, 16)

            @block.gpsimd
            def _(pool):
                tail.pool_setup()
                nc.gpsimd.memset(zero[:], 0.0).then_inc(s_zero, 1)
                with pool.Fori(0, BATCH) as b:
                    for c in range(NC):
                        tail.pool_rstd(pool, b, c)

            @block.scalar
            def _(act):
                tail.act_setup(act)

                def turn(t, post):
                    for c in range(NC + 1):
                        if c == 1 and post is not None:
                            tail.act_exp(act, post)
                        if c < NC:
                            tail.act_norm(act, t, c)
                        if c >= 1:
                            tail.act_evac(act, t, c - 1)

                turn(0, None)
                with act.Fori(0, BATCH - 1) as b:
                    turn(b + 1, b)
                tail.act_exp(act, BATCH - 1)

            @block.vector
            def _(dve):
                dve.wait_ge(s_const, 48)
                tail.dve_setup()

                def turn(t, post):
                    for c in range(NC):
                        if c % 2 == 0:
                            dve.wait_ge(s_x[c // 2], t * 16 + 16)
                        tail.dve_stats(dve, t, c)
                        if post is not None and c < 7:
                            tail.post(dve, post, c)
                    tail.dve_keep(dve, t)

                turn(0, None)
                dve.wait_ge(s_prep, 1)
                dve.tensor_copy(WT[:], ps[:, 5, :].rearrange("p (a b) -> p a b", a=2)).then_inc(s_prepd, 1)
                dve.tensor_scalar(WIN[:, 4:6, :], WIN[:, 4:6, :], DV[:, 0:1], None, ALU.mult).then_inc(s_prepd, 1)
                dve.wait_ge(s_prepd, 2)
                dve.tensor_copy(WOUT[:, 0:2, :], WT[:])
                dve.tensor_copy(WOUT[:, 4:6, :], WIN[:, 4:6, :]).then_inc(s_prepd, 1)
                dve.wait_ge(s_prepd, 3)
                dve.tensor_tensor(WOUT[:, 2:4, :], WT[:], WOUT[:, 0:2, :].bitcast(F32), ALU.subtract).then_inc(s_prepd, 1)
                dve.tensor_tensor(WOUT[:, 6:8, :], WIN[:, 4:6, :], WOUT[:, 4:6, :].bitcast(F32),
                                  ALU.subtract).then_inc(s_prepd, 1)
                with dve.Fori(0, BATCH - 1) as b:
                    turn(b + 1, b)
                for k in range(7):
                    tail.post(dve, BATCH - 1, k)
                tail.dve_finish(dve)

            @block.tensor
            def _(pe):
                pe.wait_ge(s_const, 48)
                tail.pe_setup(pe)
                pe.wait_ge(s_w, 64)
                for kh in range(HC):
                    for j in range(HC):
                        ins = pe.matmul(ps[:, 5, kh * H:(kh + 1) * H], WIN[:, j, kh * P:(kh + 1) * P], WIN[:, 2 + j, :],
                                        start=(j == 0), stop=(j == HC - 1))
                ins.then_inc(s_prep, 1)

                def turn(t, post):
                    for c in range(NC + 1):
                        if c < NC:
                            tail.pe_turn(pe, t, c)
                        if c >= 1:
                            tail.pe_logits(pe, t, c - 1)
                        if post is not None:
                            if c == 1:
                                tail.pe_count(pe, post)
                            if c >= 4 and c < 8:
                                tail.pe_inv(pe, post, c - 4)

                turn(0, None)
                with pe.Fori(0, BATCH - 1) as b:
                    turn(b + 1, b)
                tail.pe_count(pe, BATCH - 1)
                for q in range(4):
                    tail.pe_inv(pe, BATCH - 1, q)
                tail.pe_finish(pe)

        def experts(tag):
            with ExitStack() as st:
                NQ = (ET + 1) // 2
                WRAW = sb([P, 6, F], F32, st, "wraw")
                WS = sb([P, 2, 2, 6, F], F32R, st, "ws")
                IDX = sb([P, 2, ET], U32, st, "idx")
                XG = sb([P, 2, ET, H], F32, st, "xg")
                XS = sb([P, 2, HC, CAP], F32R, st, "xs")
                SG = sb([P, 2, SL], F32, st, "sg")
                HF = sb([P, 2, SL], F32, st, "hf")
                HS = sb([P, 2, HC, CAP], F32R, st, "hs")
                YS = sb([P, ET, H], F32, st, "ys")
                w_in = [sem(f"{tag}_w_in")]
                xg_in = [sem(f"{tag}_xg_in{r}") for r in range(2)]
                y_out = sem(f"{tag}_y_out")
                whi = count(f"{tag}_whi", 3)
                wlo = count(f"{tag}_wlo", 3, 1)
                idx = count(f"{tag}_idx", 1)
                turned = count(f"{tag}_turned", NQ, 2 * NQ)
                xhi = count(f"{tag}_xhi", NQ)
                xlo = count(f"{tag}_xlo", NQ, 2)
                gu = count(f"{tag}_gu", 4, 4)
                silu = count(f"{tag}_silu", 4)
                hm = count(f"{tag}_h", 4, 2)
                hhi = count(f"{tag}_hhi", 4)
                hlo = count(f"{tag}_hlo", 4, 2)
                yd = count(f"{tag}_y", NQ, 2 * NQ)
                ycp = count(f"{tag}_ycopy", NQ, 2)
                block = st.enter_context(nc.Block())
                widths = [min(2, ET - 2 * q) * P for q in range(NQ)]

                def loop(eng, body, first=None):
                    with eng.Fori(0, E // 2 - 1) as i:
                        body(i * 2, 0, True)
                        body(i * 2 + 1, 1, True)
                    body(E - 2, 0, True)
                    body(E - 1, 1, False)

                @block.sync
                def _(sp):
                    views = [w.rearrange("e (a p) f -> e p a f", p=P) for w in (w_gate, w_up, w_down)]

                    def weights(e):
                        wlo.wait(sp, e, 0)
                        for k, v in enumerate(views):
                            sp.dma_start(WRAW[:, 2 * k:2 * k + 2, :], v[e]).then_inc(w_in[0], 16)

                    weights(0)
                    with sp.Fori(1, E) as e:
                        weights(e)

                @block.gpsimd
                def _(pool):
                    def gather(e, r):
                        turned.wait(pool, e, -NQ)
                        idx.wait_apart(pool, e, 1)
                        for k in range(ET):
                            nc.gpsimd.indirect_dma_start(
                                out=XG[:, r, k, :], out_offset=None, in_=xn_rows,
                                in_offset=bass.IndirectOffsetOnAxis(ap=IDX[:, r, k:k + 1], axis=0),
                            ).then_inc(xg_in[r], 16)

                    with pool.Fori(0, E // 2) as i:
                        gather(i * 2, 0)
                        gather(i * 2 + 1, 1)

                @block.scalar
                def _(act):
                    ycp.grant(act)

                    def split_w(e, r, k):
                        if k == 0:
                            act.wait_ge(w_in[0], e * 48 + 48)
                            yd.wait(act, e, -NQ)
                        act.copy(WS[:, r, 0, 2 * k:2 * k + 2], WRAW[:, 2 * k:2 * k + 2]).then_inc(whi.sem, 1)

                    def x_hi(e, q):
                        turned.wait(act, e, q + 1)
                        if q == 0:
                            gu.wait(act, e, 0)
                        o = ps[:, q % 2, :].rearrange("p (a b) -> p a b", a=HC)[:, :, 0:widths[q]]
                        act.copy(XS[:, 0, :, 2 * P * q:2 * P * q + widths[q]], o).then_inc(xhi.sem, 1)

                    def h_hi(e, m):
                        hm.wait(act, e, m + 1)
                        if m == 0:
                            yd.wait(act, e, 0)
                        c, f = divmod(m, 2)
                        act.copy(HS[:, 0, f, SL * c:SL * c + SL], HF[:, m % 2, :]).then_inc(hhi.sem, 1)

                    y_out_v = y_rows[0:DROP, :].rearrange("(e t p) d -> e p t d", p=P, t=ET)

                    def body(e, r, more, stored):
                        for m in range(5):
                            if m < 4:
                                gu.wait(act, e, m + 1)
                                hm.wait(act, e, m + 1 - 2)
                                act.activation(SG[:, m % 2, :], ps[:, 2 + 2 * (m % 2), 0:SL],
                                               ACT.Silu).then_inc(silu.sem, 1)
                            if m < 3 and more:
                                split_w(e + 1, 1 - r, m)
                            if m == 4 and more:
                                for q in range(2):
                                    x_hi(e + 1, q)
                            if m >= 1:
                                h_hi(e, m - 1)
                        if more:
                            for q in range(2, NQ):
                                x_hi(e + 1, q)
                        for q in range(NQ):
                            yd.wait(act, e, q + 1)
                            if q == 0 and stored is not None:
                                act.wait_ge(y_out, stored * 16)
                            act.copy(YS[:, 2 * q:2 * q + widths[q] // P, :],
                                     ps[:, 6 + q % 2, 0:2 * widths[q]].rearrange("p (t d) -> p t d", d=H)
                                     ).then_inc(ycp.sem, 1)
                        ycp.wait(act, e, NQ)
                        act.dma_start(y_out_v[e], YS[:]).then_inc(y_out, 16)

                    nc.scalar.preload_act_table_set("silu_and_others")
                    for k in range(3):
                        split_w(0, 0, k)
                    for q in range(NQ):
                        x_hi(0, q)
                    body(0, 0, True, None)
                    body(1, 1, True, 1)
                    with act.Fori(0, E // 2 - 2) as i:
                        body(i * 2 + 2, 0, True, i * 2 + 2)
                        body(i * 2 + 3, 1, True, i * 2 + 3)
                    body(E - 2, 0, True, E - 2)
                    body(E - 1, 1, False, E - 1)
                    act.wait_ge(y_out, E * 16)

                @block.vector
                def _(dve):
                    wlo.grant(dve)
                    xlo.grant(dve)
                    hm.grant(dve)
                    hlo.grant(dve)

                    def index(e, r):
                        dve.tensor_copy(IDX[:, r, :], INV[:, bass.ds(e * ET, ET)]).then_inc(idx.sem, 1)

                    def split_w(e, r, k):
                        whi.wait(dve, e, k + 1)
                        w = slice(2 * k, 2 * k + 2)
                        dve.tensor_tensor(WS[:, r, 1, w], WRAW[:, w], WS[:, r, 0, w].bitcast(F32),
                                          ALU.subtract).then_inc(wlo.sem, 1)

                    def x_lo(e, q):
                        xhi.wait(dve, e, q + 1)
                        o = ps[:, q % 2, :].rearrange("p (a b) -> p a b", a=HC)[:, :, 0:widths[q]]
                        s = slice(2 * P * q, 2 * P * q + widths[q])
                        dve.tensor_tensor(XS[:, 1, :, s], o, XS[:, 0, :, s].bitcast(F32),
                                          ALU.subtract).then_inc(xlo.sem, 1)

                    def h_lo(e, m):
                        hhi.wait(dve, e, m + 1)
                        c, f = divmod(m, 2)
                        s = slice(SL * c, SL * c + SL)
                        dve.tensor_tensor(HS[:, 1, f, s], HF[:, m % 2, :], HS[:, 0, f, s].bitcast(F32),
                                          ALU.subtract).then_inc(hlo.sem, 1)

                    def gathered(e, r):
                        dve.wait_ge(xg_in[r], e * (8 * ET) + (2 - r) * 8 * ET)
                        apart(dve)

                    def body(e, r, more, ahead):
                        for m in range(5):
                            if m < 4:
                                silu.wait(dve, e, m + 1)
                                hlo.wait(dve, e, m - 1)
                                dve.tensor_tensor(HF[:, m % 2, :], ps[:, 3 + 2 * (m % 2), 0:SL], SG[:, m % 2, :],
                                                  ALU.mult).then_inc(hm.sem, 1)
                            if m < 3 and more:
                                split_w(e + 1, 1 - r, m)
                            if m == 0 and ahead:
                                gathered(e, r)
                                index(e + 2, r)
                            if m == 4 and more:
                                x_lo(e + 1, 0)
                            if m >= 1:
                                h_lo(e, m - 1)
                        if more:
                            for q in range(1, NQ):
                                x_lo(e + 1, q)

                    index(0, 0)
                    index(1, 1)
                    for k in range(3):
                        split_w(0, 0, k)
                    for q in range(NQ):
                        x_lo(0, q)

                    def pair(i, more):
                        body(i * 2, 0, True, more)
                        body(i * 2 + 1, 1, more, more)

                    with dve.Fori(0, E // 2 - 1) as i:
                        pair(i, True)
                    pair(E // 2 - 1, False)

                @block.tensor
                def _(pe):
                    turned.grant(pe)
                    gu.grant(pe)
                    yd.grant(pe)

                    def turn(e, r, quads):
                        if quads[0] == 0:
                            pe.wait_ge(xg_in[r], e * (8 * ET) + (2 - r) * 8 * ET)
                        for q in quads:
                            xlo.wait(pe, e, q + 1 - 2)
                            for j in range(widths[q] // P):
                                for h in range(HC):
                                    o = h * 2 * P + j * P
                                    ins = pe.transpose(ps[:, q % 2, o:o + P],
                                                       XG[:, r, 2 * q + j, h * P:(h + 1) * P], IDENT)
                            ins.then_inc(turned.sem, 1)

                    def product(dst, left, right):
                        terms = [(a, b, k) for k in range(HC) for a, b in ((0, 0), (0, 1), (1, 0))]
                        for n, (a, b, k) in enumerate(terms):
                            ins = pe.matmul(dst, left(a, k), right(b, k), start=(n == 0), stop=(n == len(terms) - 1))
                        return ins

                    def body(e, r, more):
                        wlo.wait(pe, e, 3)
                        xlo.wait(pe, e, NQ)
                        for m in range(4):
                            c, f = divmod(m, 2)
                            hm.wait(pe, e, m + 1 - 2)
                            for n in range(2):
                                ins = product(
                                    ps[:, 2 + 2 * (m % 2) + n, 0:SL],
                                    lambda a, k: WS[:, r, a, 2 * n + k, f * P:(f + 1) * P],
                                    lambda b, k: XS[:, b, k, SL * c:SL * c + SL],
                                )
                            ins.then_inc(gu.sem, 1)
                        if more:
                            turn(e + 1, 1 - r, range(2))
                        for q in range(NQ):
                            if q == 1 and more:
                                turn(e + 1, 1 - r, range(2, NQ))
                            hlo.wait(pe, e, 2 * (2 * P * q + widths[q] > SL) + 2)
                            ycp.wait(pe, e, q + 1 - 2)
                            for j in range(widths[q] // P):
                                ins = product(
                                    ps[:, 6 + q % 2, j * H:(j + 1) * H],
                                    lambda a, k: HS[:, a, k, (2 * q + j) * P:(2 * q + j + 1) * P],
                                    lambda b, k: WS[:, r, b, 4 + k, :],
                                )
                            ins.then_inc(yd.sem, 1)

                    turn(0, 0, range(NQ))
                    loop(pe, body)


        class Combine:

            def __init__(self, stack, tag, ring, more):
                self.ring = ring
                self.idx = sb([P, TB], U32, stack, "idx")
                self.gb = sb([P, TB], F32, stack, "gb")
                self.s1 = sb([P, TB], F32, stack, "s1")
                self.s2 = sb([P, TB], F32, stack, "s2")
                self.yg = sb([P, ring, CH, H], F32, stack, "yg")
                self.yg_in = [sem(f"{tag}_yg_in{r}") for r in range(ring)]
                self.ready = count(f"{tag}_idx_ready", 1)
                self.comb = count(f"{tag}_combined", NC, ring)
                self.ch = Chain(sem(f"{tag}_combine"), 1 + NC * 2 + more)

            def dve_begin(self, dve, a):
                self.ch.begin(a)
                b = bass.ds(TB * a, TB)
                dve.tensor_copy(self.idx[:], SLOT[:, b])
                dve.tensor_copy(self.gb[:], GATE[:, b])
                dve.tensor_scalar(self.s2[:], NMR[:, b], 0.5, None, ALU.mult)
                self.ch.link(dve, dve.tensor_scalar(self.s1[:], RSTD[:, b], 0.5, 1.0, ALU.mult, ALU.add))
                dve.sem_inc(self.ready.sem, 1)

            def pool_gather(self, pool, a, k):
                self.ready.wait(pool, a, 1)
                self.comb.wait_apart(pool, a, k + 1 - self.ring)
                for j in range(CH):
                    nc.gpsimd.indirect_dma_start(
                        out=self.yg[:, k % self.ring, j, :], out_offset=None, in_=y_rows,
                        in_offset=bass.IndirectOffsetOnAxis(ap=self.idx[:, CH * k + j:CH * k + j + 1], axis=0),
                    ).then_inc(self.yg_in[k % self.ring], 16)

            def dve(self, dve, a, k):
                for j in range(CH):
                    c = CH * k + j
                    x_t = X[:, TB * a + c, :]
                    ins = dve.tensor_scalar(x_t, x_t, self.s1[:, c:c + 1], self.s2[:, c:c + 1], ALU.mult, ALU.add)
                self.ch.link(dve, ins)
                dve.wait_ge(self.yg_in[k % self.ring],
                            a * (16 * CH * NC // self.ring) + 16 * CH * (k // self.ring + 1))
                for j in range(CH):
                    c = CH * k + j
                    x_t = X[:, TB * a + c, :]
                    ins = dve.scalar_tensor_tensor(x_t, self.yg[:, k % self.ring, j, :], self.gb[:, c:c + 1], x_t,
                                                   ALU.mult, ALU.add)
                self.ch.link(dve, ins)
                dve.sem_inc(self.comb.sem, 1)

        def attention():
            with ExitStack() as st:
                BG, BX, BY = 0, 1, 3
                BZ = (2, 6)
                tail = Tail(st, "p3", (4, 5, 5, 7), 1, 2)
                comb = Combine(st, "p3", 2, NC)
                s = lambda shape, dt=F32, name="a": sb(shape, dt, st, name)
                WA = s([P, 8, H], F32R)
                WC, WCT = s([P, HC, H]), s([P, HC, H])
                VEC = s([P, 6, HC])
                A1, B1, BD, NBD, ABD = (VEC[:, k, :] for k in range(5))
                RA, NA, RB, NB = s([P, TB]), s([P, TB]), s([P, TB]), s([P, TB])
                BSA, MVA, MRA, VEA = s([P, 2, CH, 6]), s([P, 2, CH, 2]), s([P, CH]), s([P, CH])
                XA = s([P, 2, CH, H + 1])
                XB = s([P, 2, CH, H])
                XS = s([P, 3, 2, HC, CT], F32R)
                AB = s([P, 2, HC, CT])
                CC = s([P, 2, HC, CT])
                YT = s([P, 2, HC, CT])
                TMP = s([P, HC, CT])
                NG = H + 1 + P + 1
                GS = s([P, NG])
                UV = s([P, 5, HC])
                s_w, s_set = sem("p3_w_in"), sem("p3_setup")
                stats = count("a_stats", NC)
                rstd = count("a_rstd", NC, 2)
                normed = count("a_normed", NC, 1)
                gd = count("a_gram", NC, 2)
                gs = count("a_gram_read", 2, 1)
                ucd = count("a_sums", 1)
                xbd = count("b_norm", NC)
                tb = count("b_turned", NC, 2)
                hi = count("b_hi", NC)
                lo = count("b_lo", NC, 1)
                zd = count("b_z", NC)
                lnd = count("b_log", NC)
                dz = count("b_softplus", NC, 2)
                scn = count("b_scan", NC, 2)
                e2d = count("b_da", NC, 2)
                yd = count("b_y", NC)
                yr = count("b_residual", NC, 2)
                x2 = count("b_x", NC, 1)
                ach = Chain(sem("a_pool"), 3 * NC)
                bch = Chain(sem("b_dve"), 1 + NC + 3)
                cch = Chain(sem("b_act"), 2 * NC)
                block = st.enter_context(nc.Block())
                MID = BATCH - 2

                STEPS = NC + 5
                A_AT = (1, 2, 7, 8, 9, 10, 11, 11)
                HOT_AT = {3: 3, 4: 9, 5: 10, 6: 11}

                def a_at(s):
                    return [k for k in range(NC) if A_AT[k] == s]

                def turns(eng, body, last):
                    body(0, 1, None)
                    with eng.Fori(0, MID) as i:
                        body(i + 1, i + 2, i)
                    body(BATCH - 1, None, BATCH - 2)
                    last()

                @block.sync
                def _(sp):
                    tail.sp_setup()
                    sp.dma_start(WA[:].bitcast(F32).rearrange("p a b -> p (a b)"), w_ready).then_inc(s_w, 16)
                    for dst, src in ((WC, w_c), (WCT, w_c_t)):
                        sp.dma_start(dst[:], src.rearrange("(a p) e -> p a e", p=P)).then_inc(s_w, 16)
                    for k, v in enumerate((a_vec, b_vec, b_delta)):
                        sp.dma_start(VEC[:, k, :], v).then_inc(s_w, 16)
                    with sp.Fori(0, BATCH) as t:
                        for c in range(NC):
                            tail.sp_store(sp, t, c)

                @block.gpsimd
                def _(pool):
                    tail.pool_setup()
                    rstd.grant(pool)

                    def a_rstd(a, k):
                        if k == 0:
                            ach.begin(a)
                            normed.wait(pool, a, 0)
                        stats.wait_apart(pool, a, k + 1)
                        c = slice(CH * k, CH * k + CH)
                        mean, var = MVA[:, k % 2, :, 0], MVA[:, k % 2, :, 1]
                        ach.link(pool, nc.gpsimd.tensor_scalar(VEA[:], var, EPS, None, ALU.add))
                        ach.link(pool, nc.gpsimd.tensor_tensor(RA[:, c], VEA[:], NHALF, ALU.pow))
                        ach.link(pool, nc.gpsimd.tensor_tensor(MRA[:], mean, RA[:, c], ALU.mult), alone=True)
                        nc.gpsimd.tensor_scalar(NA[:, c], MRA[:], -1.0, None, ALU.mult).then_inc(rstd.sem, 1)

                    def body(t, a, p):
                        if a is not None:
                            for k in range(2):
                                comb.pool_gather(pool, a, k)
                        for s in range(STEPS):
                            if a is not None:
                                for k in a_at(s):
                                    a_rstd(a, k)
                                    if k + 2 < NC:
                                        comb.pool_gather(pool, a, k + 2)
                            if 3 <= s < NC + 3:
                                tail.pool_rstd(pool, t, s - 3)

                    for k in range(2):
                        comb.pool_gather(pool, 0, k)
                    for k in range(NC):
                        a_rstd(0, k)
                        if k + 2 < NC:
                            comb.pool_gather(pool, 0, k + 2)
                    turns(pool, body, lambda: None)

                @block.scalar
                def _(act):
                    tail.act_setup(act)
                    normed.grant(act)
                    e2d.grant(act)
                    act.wait_ge(s_w, 96)
                    act.wait_ge(s_set, 2)

                    def a_norm(a, k):
                        gd.wait(act, a, k - 1)
                        rstd.wait_apart(act, a, k + 1)
                        for j in range(CH):
                            c = CH * k + j
                            ins = act.activation(XA[:, k % 2, j, 0:H], X[:, TB * a + c, :], ACT.Identity,
                                                 bias=NA[:, c:c + 1], scale=RA[:, c:c + 1])
                        ins.then_inc(normed.sem, 1)

                    def x_hi(t, s):
                        tb.wait(act, t, s + 1)
                        yr.wait(act, t, max(s - 2, 0))
                        act.copy(XS[:, s % 3, 0].rearrange("p a b -> p (a b)"), ps[:, BX, :]).then_inc(hi.sem, 1)

                    def softplus(t, s):
                        if s == 0:
                            cch.begin(t)
                        zd.wait(act, t, s + 1)
                        scn.wait(act, t, s - 1)
                        e2d.wait(act, t, s - 1)
                        for h in range(HC):
                            ins = act.activation(AB[:, s % 2, h, :], ps[:, BZ[s % 2], h * CT:(h + 1) * CT], ACT.Abs,
                                                 bias=BD[:, h:h + 1])
                        cch.link(act, ins)
                        cch.link(act, act.activation(AB[:, s % 2], AB[:, s % 2], ACT.Exp, scale=-1.0))
                        act.activation(AB[:, s % 2], AB[:, s % 2], ACT.Ln, bias=1.0).then_inc(lnd.sem, 1)

                    def d_a(t, s):
                        dz.wait(act, t, s + 1)
                        yr.wait(act, t, s - 1)
                        for h in range(HC):
                            ins = act.activation(YT[:, s % 2, h, :], AB[:, s % 2, h, :], ACT.Exp,
                                                 bias=ABD[:, h:h + 1], scale=A1[:, h:h + 1])
                        ins.then_inc(e2d.sem, 1)

                    def body(t, a, p):
                        for s in range(STEPS):
                            if 2 <= s < NC + 2:
                                d_a(t, s - 2)
                            if s < NC:
                                x_hi(t, s)
                            if 4 <= s < NC + 4:
                                tail.act_norm(act, t, s - 4)
                            if s == 0 and p is not None:
                                tail.act_exp(act, p)
                            if 1 <= s <= NC:
                                softplus(t, s - 1)
                            if 4 <= s < NC + 4:
                                tail.act_evac(act, t, s - 4)
                            if a is not None:
                                for k in a_at(s):
                                    a_norm(a, k)

                    nc.scalar.preload_act_table_set("natural_log_exp_and_others")
                    for k in range(NC):
                        a_norm(0, k)
                    turns(act, body, lambda: tail.act_exp(act, BATCH - 1))

                @block.vector
                def _(dve):
                    for c in (gs, lo, dz, scn, x2, comb.comb):
                        c.grant(dve)
                    tail.dve_setup()
                    dve.memset(XA[:, :, :, H:H + 1], 1.0)
                    dve.wait_ge(s_w, 96)
                    dve.tensor_scalar(NBD, BD, -1.0, None, ALU.mult).then_inc(s_set, 1)
                    dve.tensor_tensor(ABD, A1, BD, ALU.mult).then_inc(s_set, 1)
                    dve.wait_ge(s_set, 2)

                    def a_chunk(a, k):
                        comb.dve(dve, a, k)
                        rstd.wait_apart(dve, a, k - 1)
                        for j in range(CH):
                            ins = dve.bn_stats(BSA[:, k % 2, j, :], X[:, TB * a + (CH * k + j), :])
                        comb.ch.link(dve, ins, alone=True)
                        for j in range(CH):
                            ins = dve.bn_aggr(MVA[:, k % 2, j, :], BSA[:, k % 2, j, :])
                        ins.then_inc(stats.sem, 1)

                    def a_sums(a):
                        gd.wait(dve, a, NC)
                        dve.tensor_copy(GS[:], ps[:, BG, 0:NG]).then_inc(gs.sem, 1)

                    def a_factors(a):
                        ucd.wait(dve, a, 1)
                        sums = ps[:, BG, :]
                        scratch = TMP[:].rearrange("p a b -> p (a b)")
                        for n, (l, r) in enumerate(((WC[:, 0, :], GS[:, 0:H]), (WC[:, 1, 0:P], sums[:, 0:P]),
                                                    (WC[:, 1, P:H], GS[:, H + 1:H + 1 + P]))):
                            o = (0, H, H + P)[n]
                            ins = dve.tensor_tensor_reduce(out=scratch[:, o:o + l.shape[1]], in0=l, in1=r, scale=1.0,
                                                           scalar=0.0, op0=ALU.mult, op1=ALU.add,
                                                           accum_out=UV[:, 2 + n // 2, n % 2:n % 2 + 1])
                        bch.link(dve, ins)
                        bch.link(dve, dve.tensor_tensor(UV[:, 2, 1:2], UV[:, 2, 1:2], UV[:, 3, 0:1], ALU.add))
                        dve.tensor_tensor(UV[:, 0, :], UV[:, 2, :], B1, ALU.mult)
                        bch.link(dve, dve.tensor_tensor(UV[:, 1, :], sums[:, P:P + HC], B1, ALU.mult))
                        dve.sem_inc(gs.sem, 1)

                    def b_norm(t, s):
                        tb.wait(dve, t, s - 1)
                        for j in range(CH):
                            c = CH * s + j
                            ins = dve.tensor_scalar(XB[:, s % 2, j, :], X[:, TB * t + c, :], RB[:, c:c + 1],
                                                    NB[:, c:c + 1], ALU.mult, ALU.add)
                        ins.then_inc(xbd.sem, 1)

                    def x_lo(t, s):
                        hi.wait(dve, t, s + 1)
                        dve.tensor_tensor(XS[:, s % 3, 1].rearrange("p a b -> p (a b)"), ps[:, BX, :],
                                          XS[:, s % 3, 0].bitcast(F32).rearrange("p a b -> p (a b)"),
                                          ALU.subtract).then_inc(lo.sem, 1)

                    def y(t, s):
                        e2d.wait(dve, t, s + 1)
                        scn.wait(dve, t, s + 1)
                        for h in range(HC):
                            ins = dve.tensor_scalar(TMP[:, h, :], CC[:, s % 2, h, :], UV[:, 1, h:h + 1], None, ALU.mult)
                        bch.link(dve, ins)
                        for h in range(HC):
                            ins = dve.scalar_tensor_tensor(YT[:, s % 2, h, :], YT[:, s % 2, h, :], UV[:, 0, h:h + 1],
                                                           TMP[:, h, :], ALU.mult, ALU.add)
                        ins.then_inc(yd.sem, 1)

                    def scan(t, s):
                        lnd.wait(dve, t, s + 1)
                        for h in range(HC):
                            ins = dve.scalar_tensor_tensor(AB[:, s % 2, h, :], ps[:, BZ[s % 2], h * CT:(h + 1) * CT],
                                                           NBD[:, h:h + 1], AB[:, s % 2, h, :], ALU.max, ALU.add)
                        ins.then_inc(dz.sem, 1)
                        dz.wait(dve, t, s + 1)
                        scn.wait(dve, t, s)
                        for h in range(HC):
                            start = 0.0 if s == 0 else CC[:, 1 - s % 2, h, CT - 1:CT]
                            ins = dve.tensor_tensor_scan(CC[:, s % 2, h, :], BD[:, h:h + 1].to_broadcast([P, CT]),
                                                         AB[:, s % 2, h, :], start, ALU.add, ALU.add)
                        ins.then_inc(scn.sem, 1)

                    def x_new(t, s):
                        yr.wait(dve, t, s + 1)
                        x_t = X[:, bass.ds(TB * t + CH * s, CH), :].rearrange("p a b -> p (a b)")
                        dve.tensor_tensor(x_t, x_t, ps[:, BY, :], ALU.add).then_inc(x2.sem, 1)
                        x2.wait(dve, t, s + 1)

                    def body(t, a, p):
                        bch.begin(t)
                        rstd.wait(dve, t, NC)
                        dve.tensor_copy(RB[:], RA[:])
                        bch.link(dve, dve.tensor_copy(NB[:], NA[:]))
                        b_norm(t, 0)
                        a_sums(t)
                        if a is not None:
                            comb.dve_begin(dve, a)
                        for s in range(STEPS):
                            if 1 <= s <= NC:
                                x_lo(t, s - 1)
                            if s < NC - 1:
                                b_norm(t, s + 1)
                            if s == 1:
                                a_factors(t)
                            if 2 <= s < NC + 2:
                                scan(t, s - 2)
                            if a is not None:
                                for k in a_at(s):
                                    a_chunk(a, k)
                            if 2 <= s < NC + 2:
                                y(t, s - 2)
                            if 3 <= s < NC + 3:
                                x_new(t, s - 3)
                                tail.dve_stats(dve, t, s - 3)
                            if p is not None:
                                for q in range(7):
                                    if HOT_AT.get(q, q) == s:
                                        tail.post(dve, p, q)
                        tail.dve_keep(dve, t)
                        bch.end()
                        if a is not None:
                            comb.ch.end()

                    comb.dve_begin(dve, 0)
                    for k in range(NC):
                        a_chunk(0, k)
                    comb.ch.end()

                    def rest():
                        for k in range(7):
                            tail.post(dve, BATCH - 1, k)
                        tail.dve_finish(dve)

                    turns(dve, body, rest)

                @block.tensor
                def _(pe):
                    tail.pe_setup(pe)
                    for c in (gd, tb, yr):
                        c.grant(pe)
                    pe.wait_ge(s_w, 96)

                    def gram(a, k):
                        normed.wait(pe, a, k + 1)
                        if k == 0:
                            gs.wait(pe, a, 0)
                        for j in range(CH):
                            x_c = XA[:, k % 2, j, :]
                            first = k == 0 and j == 0
                            end = k == NC - 1 and j == CH - 1
                            pe.matmul(ps[:, BG, 0:H + 1], x_c[:, 0:P], x_c, start=first, stop=end,
                                      skip_group_check=True)
                            ins = pe.matmul(ps[:, BG, H + 1:NG], x_c[:, P:H], x_c[:, P:H + 1], start=False, stop=end,
                                            skip_group_check=True)
                        ins.then_inc(gd.sem, 1)

                    def sums(a):
                        gs.wait(pe, a, 1)
                        pe.transpose(ps[:, BG, 0:P], GS[:, P:H], IDENT)
                        for h in range(HC):
                            for k in range(HC):
                                ins = pe.matmul(ps[:, BG, P + h:P + h + 1], WCT[:, k, h * P:(h + 1) * P],
                                                GS[:, (H, NG - 1)[k]:(H, NG - 1)[k] + 1], start=(k == 0),
                                                stop=(k == HC - 1))
                        ins.then_inc(ucd.sem, 1)

                    def turn(t, s):
                        xbd.wait(pe, t, s + 1)
                        lo.wait(pe, t, s)
                        for h in range(HC):
                            for j in range(CH):
                                o = h * CT + j * P
                                ins = pe.transpose(ps[:, BX, o:o + P], XB[:, s % 2, j, h * P:(h + 1) * P], IDENT)
                        ins.then_inc(tb.sem, 1)

                    terms = [(a, b, k) for k in range(HC) for a, b in ((0, 0), (0, 1), (1, 0))]

                    def delta(t, s):
                        lo.wait(pe, t, s + 1)
                        dz.wait(pe, t, s - 1)
                        for h in range(HC):
                            for n, (a, b, k) in enumerate(terms):
                                ins = pe.matmul(ps[:, BZ[s % 2], h * CT:(h + 1) * CT], WA[:, 2 * a + k, h * P:(h + 1) * P],
                                                XS[:, s % 3, b, k, :], start=(n == 0), stop=(n == len(terms) - 1))
                        ins.then_inc(zd.sem, 1)

                    def residual(t, s):
                        yd.wait(pe, t, s + 1)
                        x2.wait(pe, t, s)
                        for j in range(CH):
                            for n, (a, b, k) in enumerate(terms):
                                pe.matmul(ps[:, BY, j * H:(j + 1) * H], XS[:, s % 3, a, k, j * P:(j + 1) * P],
                                          WA[:, 4 + 2 * b + k, :], start=(n == 0), stop=False, skip_group_check=True)
                            for h in range(HC):
                                ins = pe.matmul(ps[:, BY, j * H + h * P:j * H + (h + 1) * P],
                                                YT[:, s % 2, h, j * P:(j + 1) * P], IDENT, is_transpose=True,
                                                start=False, stop=(h == HC - 1), skip_group_check=True)
                        ins.then_inc(yr.sem, 1)

                    def body(t, a, p):
                        for s in range(STEPS):
                            if s < NC:
                                turn(t, s)
                            if s == 0:
                                sums(t)
                            if 3 <= s < NC + 3:
                                residual(t, s - 3)
                            if 1 <= s <= NC:
                                delta(t, s - 1)
                            if 5 <= s < NC + 5:
                                tail.pe_logits(pe, t, s - 5)
                            if 4 <= s < NC + 4:
                                tail.pe_turn(pe, t, s - 4)
                            if p is not None and s == 1:
                                tail.pe_count(pe, p)
                            if a is not None:
                                for k in a_at(s - 1):
                                    gram(a, k)
                            if p is not None:
                                for q in range(3, 7):
                                    if HOT_AT[q] == s - 1:
                                        tail.pe_inv(pe, p, q - 3)

                    for k in range(NC):
                        gram(0, k)

                    def rest():
                        tail.pe_count(pe, BATCH - 1)
                        for q in range(4):
                            tail.pe_inv(pe, BATCH - 1, q)
                        tail.pe_finish(pe)

                    turns(pe, body, rest)

        def finish():
            with ExitStack() as st:
                comb = Combine(st, "p5", 8, 0)
                s_out = sem("out_stored")
                block = st.enter_context(nc.Block())
                rows = out.rearrange("(b k j p) d -> b k p j d", p=P, j=CH, k=NC)

                @block.sync
                def _(sp):
                    with sp.Fori(0, BATCH) as a:
                        for k in range(NC):
                            comb.comb.wait(sp, a, k + 1)
                            sp.dma_start(rows[a, k], X[:, bass.ds(TB * a + CH * k, CH), :]).then_inc(s_out, 16)
                    sp.wait_ge(s_out, 16 * BATCH * NC)

                @block.gpsimd
                def _(pool):
                    with pool.Fori(0, BATCH) as a:
                        for k in range(NC):
                            comb.pool_gather(pool, a, k)

                @block.vector
                def _(dve):
                    comb.comb.grant(dve)
                    with dve.Fori(0, BATCH) as a:
                        comb.dve_begin(dve, a)
                        for k in range(NC):
                            comb.dve(dve, a, k)
                        comb.ch.end()

        experts("p2")
        attention()
        experts("p4")
        finish()


_ARRAYS = ["x", "w_proj0", "w_delta_t", "w_c", "w_c_t", "w_r_t", "a_vec", "b_vec", "d_vec", "b_delta",
           "w_router", "w_gate", "w_up", "w_down", "c_f32", "c_bf16"]


def kernel(L0_attn_x, L0_attn_W_proj, L0_attn_A, L0_attn_Bp, L0_attn_D, L0_attn_W_delta, L0_attn_b_delta,
           L0_ffn_w_router, L0_ffn_w_gate, L0_ffn_w_up, L0_ffn_w_down):
    import concourse.bacc as bacc
    import ml_dtypes
    import numpy as np
    from concourse.bass_utils import run_bass_kernel_spmd

    def c(a):
        return np.ascontiguousarray(a)

    def halves(v):
        return c(np.asarray(v).reshape(HC, P).T)

    w = np.asarray(L0_attn_W_proj)
    i, f = np.arange(P), np.float32
    c_f32 = np.concatenate([np.eye(P, dtype=f), np.tile((E - np.arange(E)).astype(f), (P, 1)),
                            i[:, None].astype(f), np.tile(np.arange(TB).astype(f), (P, 1)),
                            np.full((P, CH), -0.5, f)], axis=1)
    c_bf16 = np.concatenate([(i[:, None] <= i[None, :]).astype(f), np.ones((P, P), f), np.tile(i.astype(f), (P, 1)),
                             np.tile(np.arange(ST).astype(f), (P, 1)), np.zeros((P, P), f)],
                            axis=1).astype(ml_dtypes.bfloat16)
    arrays = dict(
        x=c(np.asarray(L0_attn_x).reshape(T, H)), w_proj0=c(w[0:H]), w_delta_t=c(np.asarray(L0_attn_W_delta).T),
        w_c=c(w[2 * H:3 * H]), w_c_t=c(w[2 * H:3 * H].T), w_r_t=c(w[3 * H:4 * H].T), a_vec=halves(L0_attn_A),
        b_vec=halves(L0_attn_Bp), d_vec=c(np.broadcast_to(np.asarray(L0_attn_D).reshape(1, 1), (P, 1))),
        b_delta=halves(L0_attn_b_delta), w_router=c(L0_ffn_w_router), w_gate=c(L0_ffn_w_gate),
        w_up=c(L0_ffn_w_up), w_down=c(L0_ffn_w_down), c_f32=c_f32, c_bf16=c_bf16)
    nc = bacc.Bacc("TRN2", target_bir_lowering=False, num_devices=1)
    feeds, args = {}, []
    for name in _ARRAYS:
        a = arrays[name]
        feeds[f"in_{name}"] = a
        args.append(nc.dram_tensor(f"in_{name}", a.shape, mybir.dt.from_np(a.dtype), kind="ExternalInput").ap())
    out = nc.dram_tensor("out", [T, H], F32, kind="ExternalOutput").ap()
    macaron(nc, *args, out)
    r = run_bass_kernel_spmd(nc, [feeds], core_ids=[0])
    return r.results[0]["out"].reshape(BATCH, SEQ, H)
```

```python
from contextlib import ExitStack

import concourse.bass as bass
from concourse import mybir

ALU = mybir.AluOpType
ACT = mybir.ActivationFunctionType
AX = mybir.AxisListType.X
F32 = mybir.dt.float32
F32R = mybir.dt.float32r
BF16 = mybir.dt.bfloat16
U32 = mybir.dt.uint32

P = 128
H = 256
HC = H // P
E = 32
F = 256
BATCH, SEQ = 8, 2048
T = BATCH * SEQ
NT = T // P
TB = SEQ // P
CAP = -(-5 * T // (4 * E))
ET = CAP // P
ST = E * ET
DROP = E * CAP
CH = 2
NC = TB // CH
CT = CH * P
EPS = 1e-5
SL = CAP // 2
assert CAP % P == 0 and SL >= 256 and SL <= 512


PASSED = {}


def apart(eng):
    eng.sem_inc(PASSED[eng.engine], 1)


class Count:

    def __init__(self, sem, per, credit=0):
        self.sem, self.per, self.credit = sem, per, credit

    def at(self, turn, n):
        assert n + self.credit >= 1
        return turn * self.per + (n + self.credit)

    def grant(self, eng):
        eng.sem_inc(self.sem, self.credit)


class Chain:

    def __init__(self, sem, per):
        self.sem, self.per = sem, per
        self.turn, self.n = 0, 0

    def begin(self, turn, n=0):
        self.turn, self.n = turn, n

    def next(self):
        self.n += 1
        assert self.n <= self.per
        return self.turn * self.per + self.n

    def at(self, turn, n):
        assert 1 <= n <= self.per
        return turn * self.per + n

    def end(self):
        assert self.n == self.per, (self.n, self.per)


def macaron(nc, x, w_proj0, w_delta_t, w_c, w_c_t, w_r_t, a_vec, b_vec, d_vec, b_delta,
            w_router, w_gate, w_up, w_down, c_f32, c_bf16, out):
    with ExitStack() as ctx:
        names = [0]

        def sb(shape, dt=F32, stack=ctx, name="t"):
            names[0] += 1
            return stack.enter_context(nc.sbuf_tensor(f"{name}_{names[0]}", shape, dt))

        def sem(name):
            names[0] += 1
            return ctx.enter_context(nc.semaphore(f"{name}_{names[0]}"))

        def count(name, per, credit=0):
            return Count(sem(name), per, credit)

        for eng in (nc.vector, nc.scalar, nc.gpsimd):
            PASSED[eng.engine] = sem("passed")

        xn_rows = nc.dram_tensor("xn_rows", [T, H], F32, kind="Internal").ap()
        y_rows = nc.dram_tensor("y_rows", [T + DROP, H], F32, kind="Internal").ap()
        w_ready = nc.dram_tensor("w_ready", [P, 8 * H], F32, kind="Internal").ap()

        ps = ctx.enter_context(nc.psum_tensor("ps", [P, 8, 512], F32))

        X = sb([P, NT, H], name="x")
        RSTD = sb([P, NT], name="rstd")
        NMR = sb([P, NT], name="nmr")
        GATE = sb([P, NT], name="gate")
        INV = sb([P, ST], U32, name="inv")
        DEST = sb([P, ST], U32, name="dest")
        CF = sb([P, 128 + 32 + 1 + 16 + CH], F32, name="cf")
        CB = sb([P, 128 * 3 + 160 + 128], BF16, name="cb")
        WR = sb([P, HC, E], F32, name="wr")
        IDENT = CF[:, 0:128]
        REV = CF[:, 128:160]
        LANE = CF[:, 160:161]
        IOTA16 = CF[:, 161:177]
        NHALF = CF[:, 177:177 + CH]
        TRI = CB[:, 0:128]
        ONES = CB[:, 128:256]
        IOTA128 = CB[:, 256:384]
        IOTA160 = CB[:, 384:544]
        BZERO = CB[:, 544:672]

        def mid(ap, n):
            return ap.unsqueeze(1).to_broadcast([P, n, ap.shape[1]])

        def last(ap, k):
            return ap.unsqueeze(2).to_broadcast([P, ap.shape[1], k])

        class Tail:

            def __init__(self, stack, tag, banks, n_t, xr):
                self.bt, self.bl, self.bc, self.bi = banks
                self.n_t, self.xr = n_t, xr
                s = lambda shape, dt=F32, name="r": sb(shape, dt, stack, name)
                self.bs = s([P, 2, CH, 6])
                self.mv = s([P, 2, CH, 2])
                self.rb = s([P, TB])
                self.nb = s([P, TB])
                self.mr = s([P, CH])
                self.ve = s([P, CH])
                self.xn = s([P, xr, CH, H])
                self.xt = s([P, 2, HC, CH, P])
                self.d = s([P, TB, E])
                self.cand = s([P, TB, E])
                self.oh = s([P, TB, E], BF16)
                self.small = s([P, 12, TB])
                self.slu = s([P, 3, TB], U32)
                self.carry = s([P, E], BF16)
                self.cr = s([P, E])
                self.hot_slot = s([P, 2, 4, P], BF16)
                self.hot_tile = s([P, 2, 4, 2, ST], BF16)
                self.inv_f = self.d[:].rearrange("p t e -> p (t e)")[:, 0:ST]
                self.inv_g = self.cand[:].rearrange("p t e -> p (t e)")[:, 0:ST]
                self.stats = count(f"{tag}_stats", NC)
                self.rdone = count(f"{tag}_rstd", NC, 2)
                self.kept = count(f"{tag}_kept", 1, 1)
                self.normed = count(f"{tag}_normed", NC, 1)
                self.stored = [sem(f"{tag}_rows_stored{k}") for k in range(xr)]
                self.free = count(f"{tag}_rows_free", NC, xr)
                self.turned = count(f"{tag}_turned", NC, xr)
                self.evac = count(f"{tag}_evac", NC, n_t)
                self.logits = count(f"{tag}_logits", NC, 2)
                self.lread = count(f"{tag}_logits_read", 1, 1)
                self.expd = count(f"{tag}_exp", 1)
                self.ohd = count(f"{tag}_onehot", 1)
                self.cnt = count(f"{tag}_count", 1)
                self.hot = count(f"{tag}_hot", 4)
                self.inv = count(f"{tag}_inv", 4, 2)
                self.inverse = sem(f"{tag}_inv_fin")
                self.stats_chain = Chain(sem(f"{tag}_dve"), NC)
                self.cread = count(f"{tag}_count_read", 1, 1)
                self.rstd_chain = Chain(sem(f"{tag}_pool"), 3 * NC)
                self.post_ch = Chain(sem(f"{tag}_post"), 14)
                self.setup_done = sem(f"{tag}_setup")

            def dve_setup(self):
                nc.vector.memset(self.carry[:], 0.0)
                nc.vector.tensor_scalar(self.small[:, 11, :], IOTA16, float(1 - TB), None,
                                        ALU.add).then_inc(self.setup_done, 1)
                nc.vector.wait_ge(self.setup_done, 1)
                self.lread.grant(nc.vector)
                self.cread.grant(nc.vector)
                self.kept.grant(nc.vector)

            def dve_stats(self, dve, t, c):
                for j in range(CH):
                    ins = dve.bn_stats(self.bs[:, c % 2, j, :], X[:, TB * t + (CH * c + j), :])
                ins.then_inc(self.stats_chain.sem, 1)

            def dve_aggr(self, dve, t, c):
                dve.wait_ge(self.rdone.sem, self.rdone.at(t, c - 1))
                dve.wait_ge(self.stats_chain.sem, self.stats_chain.at(t, c + 1))
                apart(dve)
                for j in range(CH):
                    ins = dve.bn_aggr(self.mv[:, c % 2, j, :], self.bs[:, c % 2, j, :])
                ins.then_inc(self.stats.sem, 1)

            def dve_keep(self, dve, t):
                dve.wait_ge(self.rdone.sem, self.rdone.at(t, NC))
                apart(dve)
                dve.tensor_copy(RSTD[:, bass.ds(TB * t, TB)], self.rb[:])
                dve.tensor_copy(NMR[:, bass.ds(TB * t, TB)], self.nb[:]).then_inc(self.kept.sem, 1)

            def pool_setup(self):
                self.rdone.grant(nc.gpsimd)

            def pool_rstd(self, pool, t, c):
                self.rstd_chain.begin(t, 3 * c)
                if c == 0:
                    pool.wait_ge(self.kept.sem, self.kept.at(t, 0))
                    pool.wait_ge(self.normed.sem, self.normed.at(t, 0))
                pool.wait_ge(self.stats.sem, self.stats.at(t, c + 1))
                apart(pool)
                rb = self.rb[:, CH * c:CH * c + CH]
                nb = self.nb[:, CH * c:CH * c + CH]
                mean, var = self.mv[:, c % 2, :, 0], self.mv[:, c % 2, :, 1]
                nc.gpsimd.tensor_scalar(self.ve[:], var, EPS, None, ALU.add).then_inc(self.rstd_chain.sem, 1)
                pool.wait_ge(self.rstd_chain.sem, self.rstd_chain.next())
                nc.gpsimd.tensor_tensor(rb, self.ve[:], NHALF, ALU.pow).then_inc(self.rstd_chain.sem, 1)
                pool.wait_ge(self.rstd_chain.sem, self.rstd_chain.next())
                nc.gpsimd.tensor_tensor(self.mr[:], mean, rb, ALU.mult).then_inc(self.rstd_chain.sem, 1)
                pool.wait_ge(self.rstd_chain.sem, self.rstd_chain.next())
                apart(pool)
                nc.gpsimd.tensor_scalar(nb, self.mr[:], -1.0, None, ALU.mult).then_inc(self.rdone.sem, 1)

            def act_setup(self, act):
                self.evac.grant(act)
                self.normed.grant(act)

            def act_norm(self, act, t, c):
                act.wait_ge(self.free.sem, self.free.at(t, c + 1 - self.xr))
                act.wait_ge(self.turned.sem, self.turned.at(t, c + 1 - self.xr))
                act.wait_ge(self.rdone.sem, self.rdone.at(t, c + 1))
                apart(act)
                for j in range(CH):
                    k = CH * c + j
                    ins = act.activation(self.xn[:, c % self.xr, j, :], X[:, TB * t + k, :], ACT.Identity,
                                         bias=self.nb[:, k:k + 1], scale=self.rb[:, k:k + 1])
                ins.then_inc(self.normed.sem, 1)

            def act_evac(self, act, t, c):
                act.wait_ge(self.turned.sem, self.turned.at(t, c + 1))
                act.wait_ge(self.logits.sem, self.logits.at(t, c - 1))
                act.copy(self.xt[:, c % 2].rearrange("p a b c -> p (a b c)"),
                         ps[:, self.bt + c % self.n_t, :]).then_inc(self.evac.sem, 1)

            def act_exp(self, act, p):
                act.wait_ge(self.post_ch.sem, self.post_ch.at(p, 3))
                act.activation(self.d[:], self.d[:], ACT.Exp).then_inc(self.expd.sem, 1)

            def sp_setup(self):
                self.free.grant(nc.sync)

            def sp_free(self, sp, t, c):
                sp.wait_ge(self.stored[c % self.xr], t * (16 * NC // self.xr) + 16 * (c // self.xr + 1))
                sp.sem_inc(self.free.sem, 1)

            def sp_store(self, sp, t, c):
                sp.wait_ge(self.normed.sem, self.normed.at(t, c + 1))
                rows = xn_rows.rearrange("(k j p) d -> k p j d", p=P, j=CH)
                sp.dma_start(rows[t * NC + c], self.xn[:, c % self.xr]).then_inc(self.stored[c % self.xr], 16)
                lag = self.xr // 2
                if c >= lag:
                    self.sp_free(sp, t, c - lag)
                if c == NC - 1:
                    for k in range(NC - lag, NC):
                        self.sp_free(sp, t, k)

            def pe_setup(self, pe):
                self.turned.grant(pe)
                self.logits.grant(pe)
                self.inv.grant(pe)
                for k in range(2):
                    pe.matmul(ps[:, self.bi, ST * k:ST * k + ST], BZERO, IOTA160, start=(k == 0), stop=False,
                              skip_group_check=True)

            def pe_turn(self, pe, t, c):
                pe.wait_ge(self.normed.sem, self.normed.at(t, c + 1))
                pe.wait_ge(self.evac.sem, self.evac.at(t, c + 1 - self.n_t))
                for j in range(CH):
                    for h in range(HC):
                        o = (h * CH + j) * P
                        ins = pe.transpose(ps[:, self.bt + c % self.n_t, o:o + P],
                                           self.xn[:, c % self.xr, j, h * P:(h + 1) * P], IDENT)
                ins.then_inc(self.turned.sem, 1)

            def pe_logits(self, pe, t, c):
                pe.wait_ge(self.evac.sem, self.evac.at(t, c + 1))
                if c == 0:
                    pe.wait_ge(self.lread.sem, self.lread.at(t, 0))
                for j in range(CH):
                    k = CH * c + j
                    for h in range(HC):
                        ins = pe.matmul(ps[:, self.bl, k * E:(k + 1) * E], self.xt[:, c % 2, h, j, :],
                                        WR[:, h, :], start=(h == 0), stop=(h == HC - 1))
                ins.then_inc(self.logits.sem, 1)

            def post(self, dve, p, step):
                ch, s = self.post_ch, self.small
                lg = ps[:, self.bl, :].rearrange("p (t e) -> p t e", e=E)
                ct = ps[:, self.bc, :].rearrange("p (t e) -> p t e", e=E)
                mx, rr, se, gt, ci, acc, t1, t2, slf, lo, hi, tid = (s[:, k, :] for k in range(12))
                if step == 0:
                    ch.begin(p)
                    dve.wait_ge(self.logits.sem, self.logits.at(p, NC))
                    dve.reduce_max(mx, lg, AX).then_inc(ch.sem, 1)
                    dve.wait_ge(ch.sem, ch.next())
                    dve.tensor_tensor(self.d[:], lg, last(mx, E), ALU.subtract).then_inc(ch.sem, 1)
                    dve.wait_ge(ch.sem, ch.next())
                    dve.sem_inc(self.lread.sem, 1)
                    dve.scalar_tensor_tensor(self.cand[:], self.d[:], 0.0, mid(REV, TB), ALU.is_ge,
                                             ALU.mult).then_inc(ch.sem, 1)
                    dve.wait_ge(ch.sem, ch.next())
                    dve.reduce_max(rr, self.cand[:], AX).then_inc(ch.sem, 1)
                    dve.wait_ge(ch.sem, ch.next())
                    dve.tensor_tensor(self.oh[:], mid(REV, TB), last(rr, E), ALU.is_equal).then_inc(self.ohd.sem, 1)
                if step == 1:
                    dve.wait_ge(self.expd.sem, self.expd.at(p, 1))
                    dve.reduce_sum(se, self.d[:], AX).then_inc(ch.sem, 1)
                    dve.wait_ge(ch.sem, ch.next())
                    dve.reciprocal(gt, se)
                if step == 2:
                    dve.wait_ge(self.cnt.sem, self.cnt.at(p, 1))
                    dve.tensor_tensor(self.cand[:], self.oh[:], ct, ALU.mult).then_inc(ch.sem, 1)
                    dve.wait_ge(ch.sem, ch.next())
                    dve.sem_inc(self.cread.sem, 1)
                    dve.reduce_sum(ci, self.cand[:], AX)
                    dve.reduce_sum(self.cr[:], self.oh[:].rearrange("p t e -> p e t"), AX).then_inc(ch.sem, 1)
                    dve.wait_ge(ch.sem, ch.next())
                    dve.tensor_tensor(self.carry[:], self.carry[:], self.cr[:], ALU.add)
                    dve.tensor_scalar(acc, ci, float(CAP), None, ALU.is_le)
                    dve.scalar_tensor_tensor(t1, rr, float(-CAP), ci, ALU.mult, ALU.add).then_inc(ch.sem, 1)
                    dve.wait_ge(ch.sem, ch.next())
                    dve.scalar_tensor_tensor(t2, t1, -1.0, acc, ALU.add, ALU.mult).then_inc(ch.sem, 1)
                    dve.wait_ge(ch.sem, ch.next())
                    dve.tensor_scalar(slf, t2, float(DROP), None, ALU.add).then_inc(ch.sem, 1)
                    dve.wait_ge(ch.sem, ch.next())
                    dve.tensor_copy(self.slu[:, 0, :], slf).then_inc(ch.sem, 1)
                    dve.wait_ge(ch.sem, ch.next())
                    dve.tensor_scalar(self.slu[:, 1, :], self.slu[:, 0, :], P - 1, None, ALU.bitwise_and)
                    dve.tensor_scalar(self.slu[:, 2, :], self.slu[:, 0, :], 7, None,
                                      ALU.logical_shift_right).then_inc(ch.sem, 1)
                    dve.wait_ge(ch.sem, ch.next())
                    dve.tensor_copy(lo, self.slu[:, 1, :])
                    dve.tensor_copy(hi, self.slu[:, 2, :])
                    dve.tensor_scalar(tid, tid, float(TB), None, ALU.add)
                    dve.scalar_tensor_tensor(GATE[:, bass.ds(TB * p, TB)], gt, 0.5, acc,
                                             ALU.mult, ALU.mult).then_inc(ch.sem, 1)
                    dve.wait_ge(ch.sem, ch.next())
                if step >= 3:
                    q = step - 3
                    dve.wait_ge(self.inv.sem, self.inv.at(p, q + 1 - 2))
                    for k in range(4):
                        j = 4 * q + k
                        dve.tensor_scalar(self.hot_slot[:, q % 2, k, :], IOTA128, lo[:, j:j + 1], None, ALU.is_equal)
                        dve.tensor_scalar(self.hot_tile[:, q % 2, k, 0, :], IOTA160, hi[:, j:j + 1], tid[:, j:j + 1],
                                          ALU.is_equal, ALU.mult)
                        ins = dve.tensor_scalar(self.hot_tile[:, q % 2, k, 1, :], IOTA160, hi[:, j:j + 1], LANE,
                                                ALU.is_equal, ALU.mult)
                    ins.then_inc(self.hot.sem, 1)
                if step == 6:
                    dve.wait_ge(self.hot.sem, self.hot.at(p, 4))
                    dve.sem_inc(ch.sem, 1)
                    ch.n += 1
                    ch.end()

            def pe_count(self, pe, p):
                pe.wait_ge(self.ohd.sem, self.ohd.at(p, 1))
                ct = ps[:, self.bc, :].rearrange("p (t e) -> p t e", e=E)
                pe.matmul(ct, ONES, mid(self.carry[:], TB), start=True, stop=False, skip_group_check=True)
                for j in range(TB - 1):
                    pe.matmul(ct[:, j + 1:, :], ONES, mid(self.oh[:, j, :], TB - 1 - j), start=False, stop=False,
                              skip_group_check=True)
                pe.matmul(ct, TRI, self.oh[:], start=False, stop=True,
                          skip_group_check=True).then_inc(self.cnt.sem, 1)

            def pe_inv(self, pe, p, q):
                pe.wait_ge(self.hot.sem, self.hot.at(p, q + 1))
                for k in range(4):
                    ins = pe.matmul(ps[:, self.bi, 0:2 * ST], self.hot_slot[:, q % 2, k, :], self.hot_tile[:, q % 2, k],
                                    start=False, stop=False, skip_group_check=True)
                ins.then_inc(self.inv.sem, 1)

            def pe_finish(self, pe):
                for k in range(2):
                    ins = pe.matmul(ps[:, self.bi, ST * k:ST * k + ST], BZERO, IOTA160, start=False,
                                    stop=(k == 1), skip_group_check=True)
                ins.then_inc(self.inverse, 1)

            def dve_finish(self, dve):
                dve.wait_ge(self.inverse, 1)
                dve.tensor_scalar(self.inv_f, ps[:, self.bi, ST:2 * ST], float(-P), None,
                                  ALU.add).then_inc(self.inverse, 1)
                dve.wait_ge(self.inverse, 2)
                dve.scalar_tensor_tensor(self.inv_g, ps[:, self.bi, 0:ST], float(P), self.inv_f,
                                         ALU.mult, ALU.add).then_inc(self.inverse, 1)
                dve.wait_ge(self.inverse, 3)
                dve.tensor_scalar(self.inv_f, IOTA160, float(P), LANE, ALU.mult, ALU.add).then_inc(self.inverse, 1)
                dve.wait_ge(self.inverse, 4)
                dve.tensor_scalar(self.inv_f, self.inv_f, float(T + P), None, ALU.add).then_inc(self.inverse, 1)
                dve.wait_ge(self.inverse, 5)
                dve.scalar_tensor_tensor(self.inv_f, self.inv_g, 0.0, self.inv_f, ALU.is_lt,
                                         ALU.mult).then_inc(self.inverse, 1)
                dve.wait_ge(self.inverse, 6)
                dve.tensor_tensor(self.inv_f, self.inv_f, self.inv_g, ALU.add).then_inc(self.inverse, 1)
                dve.wait_ge(self.inverse, 7)
                dve.tensor_copy(DEST[:], self.inv_f)
                dve.tensor_scalar(self.inv_g, self.inv_g, 0.0, None, ALU.max).then_inc(self.inverse, 1)
                dve.wait_ge(self.inverse, 8)
                dve.tensor_copy(INV[:], self.inv_g)

        with ExitStack() as st:
            tail = Tail(st, "p1", (0, 2, 3, 4), 2, 4)
            s_const = sem("const_in")
            s_x = [sem(f"x_in{g}") for g in range(4)]
            s_w = sem("w_in")
            s_prep, s_prepd, s_wout = sem("prep"), sem("prep_done"), sem("w_out")
            s_zero, s_zout = sem("zero"), sem("zero_out")
            WIN = sb([P, 6, H], F32, st, "win")
            WOUT = sb([P, 8, H], F32R, st, "wout")
            DV = sb([P, 1], F32, st, "dv")
            WT = sb([P, 2, H], F32, st, "wt")
            ZT = 4
            zero = sb([P, ZT, H], F32, st, "zero")
            block = st.enter_context(nc.Block())
            x_in = x.rearrange("(b g j p) d -> b g p j d", p=P, j=4, g=4)

            POST_AT = (1, 2, 4, 4, 5, 6, 7)

            def load(sp, b, g):
                sp.dma_start(X[:, bass.ds(TB * b + 4 * g, 4), :], x_in[b, g]).then_inc(s_x[g], 16)

            @block.sync
            def _(sp):
                tail.sp_setup()
                sp.dma_start(CF[:], c_f32).then_inc(s_const, 16)
                sp.dma_start(CB[:], c_bf16).then_inc(s_const, 16)
                sp.dma_start(WR[:], w_router.rearrange("(a p) e -> p a e", p=P)).then_inc(s_const, 16)
                for g in range(4):
                    load(sp, 0, g)
                for k, w in enumerate((w_proj0, w_delta_t, w_r_t)):
                    sp.dma_start(WIN[:, 2 * k:2 * k + 2, :], w.rearrange("(a p) e -> p a e", p=P)).then_inc(s_w, 16)
                sp.dma_start(DV[:], d_vec.to_broadcast([P, 1])).then_inc(s_w, 16)
                sp.wait_ge(s_zero, 1)
                zero_rows = y_rows[0:T].rearrange("(b g j p) d -> b g p j d", p=P, j=ZT, g=TB // ZT)

                def turn(t, more):
                    for c in range(NC):
                        if more and c % 2 == 0:
                            sp.wait_ge(tail.stats.sem, tail.stats.at(t, c + 2))
                            load(sp, t + 1, c // 2)
                        tail.sp_store(sp, t, c)
                        if c < TB // ZT:
                            sp.dma_start(zero_rows[t, c], zero[:]).then_inc(s_zout, 16)

                with sp.Fori(0, BATCH - 1) as b:
                    turn(b, True)
                turn(BATCH - 1, False)
                sp.wait_ge(s_prepd, 5)
                sp.dma_start(w_ready, WOUT[:].bitcast(F32).rearrange("p a b -> p (a b)")).then_inc(s_wout, 16)
                sp.wait_ge(s_wout, 16)
                sp.wait_ge(s_zout, 16 * NT // ZT)

            @block.gpsimd
            def _(pool):
                tail.pool_setup()
                nc.gpsimd.memset(zero[:], 0.0).then_inc(s_zero, 1)
                with pool.Fori(0, BATCH) as b:
                    for c in range(NC):
                        tail.pool_rstd(pool, b, c)

            @block.scalar
            def _(act):
                tail.act_setup(act)

                def turn(t, post):
                    for c in range(NC + 1):
                        if c == POST_AT[0] + 1 and post is not None:
                            tail.act_exp(act, post)
                        if c < NC:
                            tail.act_norm(act, t, c)
                        if c >= 1:
                            tail.act_evac(act, t, c - 1)

                turn(0, None)
                with act.Fori(0, BATCH - 1) as b:
                    turn(b + 1, b)
                tail.act_exp(act, BATCH - 1)

            @block.vector
            def _(dve):
                dve.wait_ge(s_const, 48)
                tail.dve_setup()

                def turn(t, post):
                    for c in range(NC):
                        if c % 2 == 0:
                            dve.wait_ge(s_x[c // 2], t * 16 + 16)
                        tail.dve_stats(dve, t, c)
                        tail.dve_aggr(dve, t, c)
                        for k in range(7):
                            if post is not None and POST_AT[k] == c:
                                tail.post(dve, post, k)
                    tail.dve_keep(dve, t)

                turn(0, None)
                dve.wait_ge(s_prep, 1)
                dve.tensor_copy(WT[:], ps[:, 5, :].rearrange("p (a b) -> p a b", a=2)).then_inc(s_prepd, 1)
                dve.tensor_scalar(WIN[:, 4:6, :], WIN[:, 4:6, :], DV[:, 0:1], None, ALU.mult).then_inc(s_prepd, 1)
                dve.wait_ge(s_prepd, 2)
                dve.tensor_copy(WOUT[:, 0:2, :], WT[:])
                dve.tensor_copy(WOUT[:, 4:6, :], WIN[:, 4:6, :]).then_inc(s_prepd, 1)
                dve.wait_ge(s_prepd, 3)
                dve.tensor_tensor(WOUT[:, 2:4, :], WT[:], WOUT[:, 0:2, :].bitcast(F32),
                                  ALU.subtract).then_inc(s_prepd, 1)
                dve.tensor_tensor(WOUT[:, 6:8, :], WIN[:, 4:6, :], WOUT[:, 4:6, :].bitcast(F32),
                                  ALU.subtract).then_inc(s_prepd, 1)
                with dve.Fori(0, BATCH - 1) as b:
                    turn(b + 1, b)
                for k in range(7):
                    tail.post(dve, BATCH - 1, k)
                tail.dve_finish(dve)

            @block.tensor
            def _(pe):
                pe.wait_ge(s_const, 48)
                tail.pe_setup(pe)
                pe.wait_ge(s_w, 64)
                for kh in range(HC):
                    for j in range(HC):
                        ins = pe.matmul(ps[:, 5, kh * H:(kh + 1) * H], WIN[:, j, kh * P:(kh + 1) * P], WIN[:, 2 + j, :],
                                        start=(j == 0), stop=(j == HC - 1))
                ins.then_inc(s_prep, 1)

                def turn(t, post):
                    for c in range(NC + 1):
                        if post is not None and c == POST_AT[0] + 1:
                            tail.pe_count(pe, post)
                        for q in range(4):
                            if post is not None and (POST_AT[3] + 1 + q, NC)[q == 3] == c:
                                tail.pe_inv(pe, post, q)
                        if c < NC:
                            tail.pe_turn(pe, t, c)
                        if c >= 1:
                            tail.pe_logits(pe, t, c - 1)

                turn(0, None)
                with pe.Fori(0, BATCH - 1) as b:
                    turn(b + 1, b)
                tail.pe_count(pe, BATCH - 1)
                for q in range(4):
                    tail.pe_inv(pe, BATCH - 1, q)
                tail.pe_finish(pe)

        def experts(tag):
            with ExitStack() as st:
                NQ = (ET + 1) // 2
                WRAW = sb([P, 6, F], F32, st, "wraw")
                WS = sb([P, 2, 2, 6, F], F32R, st, "ws")
                IDX = sb([P, 2, ET], U32, st, "idx")
                OIDX = sb([P, 2, ET], U32, st, "oidx")
                XG = sb([P, 2, ET, H], F32, st, "xg")
                XS = sb([P, 2, HC, CAP], F32R, st, "xs")
                SG = sb([P, 2, SL], F32, st, "sg")
                HF = sb([P, 2, SL], F32, st, "hf")
                HS = sb([P, 2, HC, CAP], F32R, st, "hs")
                YS = sb([P, ET, H], F32, st, "ys")
                w_in = sem(f"{tag}_w_in")
                xg_in = [sem(f"{tag}_xg_in{r}") for r in range(2)]
                y_out = sem(f"{tag}_y_out")
                whi = count(f"{tag}_whi", 3)
                wlo = count(f"{tag}_wlo", 3, 1)
                idx = count(f"{tag}_idx", 1)
                oidx = count(f"{tag}_oidx", 1)
                turned = count(f"{tag}_turned", NQ, 2 * NQ)
                xhi = count(f"{tag}_xhi", NQ)
                xlo = count(f"{tag}_xlo", NQ, 2)
                gu = count(f"{tag}_gu", 4, 4)
                silu = count(f"{tag}_silu", 4)
                hm = count(f"{tag}_h", 4, 2)
                hhi = count(f"{tag}_hhi", 4)
                hlo = count(f"{tag}_hlo", 4, 2)
                yd = count(f"{tag}_y", NQ, 2 * NQ)
                ycp = count(f"{tag}_ycopy", NQ, 2)
                block = st.enter_context(nc.Block())
                widths = [min(2, ET - 2 * q) * P for q in range(NQ)]

                def loop(eng, body, first=None):
                    with eng.Fori(0, E // 2 - 1) as i:
                        body(i * 2, 0, True)
                        body(i * 2 + 1, 1, True)
                    body(E - 2, 0, True)
                    body(E - 1, 1, False)

                @block.sync
                def _(sp):
                    views = [w.rearrange("e (a p) f -> e p a f", p=P) for w in (w_gate, w_up, w_down)]

                    def weights(e):
                        sp.wait_ge(wlo.sem, wlo.at(e, 0))
                        for k, v in enumerate(views):
                            sp.dma_start(WRAW[:, 2 * k:2 * k + 2, :], v[e]).then_inc(w_in, 16)

                    weights(0)
                    with sp.Fori(1, E) as e:
                        weights(e)

                @block.gpsimd
                def _(pool):
                    def gather(e, r):
                        pool.wait_ge(turned.sem, turned.at(e, -NQ))
                        pool.wait_ge(idx.sem, idx.at(e, 1))
                        apart(pool)
                        for k in range(ET):
                            nc.gpsimd.indirect_dma_start(
                                out=XG[:, r, k, :], out_offset=None, in_=xn_rows,
                                in_offset=bass.IndirectOffsetOnAxis(ap=IDX[:, r, k:k + 1], axis=0),
                            ).then_inc(xg_in[r], 16)

                    def scatter(e, r):
                        pool.wait_ge(oidx.sem, oidx.at(e, 1))
                        apart(pool)
                        for q in range(NQ):
                            pool.wait_ge(ycp.sem, ycp.at(e, q + 1))
                            apart(pool)
                            for k in range(2 * q, 2 * q + widths[q] // P):
                                nc.gpsimd.indirect_dma_start(
                                    out=y_rows, out_offset=bass.IndirectOffsetOnAxis(ap=OIDX[:, r, k:k + 1], axis=0),
                                    in_=YS[:, k, :], in_offset=None).then_inc(y_out, 16)

                    gather(0, 0)
                    gather(1, 1)
                    with pool.Fori(0, E // 2 - 1) as i:
                        for r in range(2):
                            gather(i * 2 + (2 + r), r)
                            scatter(i * 2 + r, r)
                    scatter(E - 2, 0)
                    scatter(E - 1, 1)

                @block.scalar
                def _(act):
                    ycp.grant(act)

                    def split_w(e, r, k):
                        if k == 0:
                            act.wait_ge(w_in, e * 48 + 48)
                            act.wait_ge(yd.sem, yd.at(e, -NQ))
                        act.copy(WS[:, r, 0, 2 * k:2 * k + 2], WRAW[:, 2 * k:2 * k + 2]).then_inc(whi.sem, 1)

                    def x_hi(e, q):
                        act.wait_ge(turned.sem, turned.at(e, q + 1))
                        if q == 0:
                            act.wait_ge(gu.sem, gu.at(e, 0))
                        o = ps[:, q % 2, :].rearrange("p (a b) -> p a b", a=HC)[:, :, 0:widths[q]]
                        act.copy(XS[:, 0, :, 2 * P * q:2 * P * q + widths[q]], o).then_inc(xhi.sem, 1)

                    def h_hi(e, m):
                        act.wait_ge(hm.sem, hm.at(e, m + 1))
                        if m == 0:
                            act.wait_ge(yd.sem, yd.at(e, 0))
                        c, f = divmod(m, 2)
                        act.copy(HS[:, 0, f, SL * c:SL * c + SL], HF[:, m % 2, :]).then_inc(hhi.sem, 1)

                    def body(e, r, more, stored):
                        for m in range(5):
                            if m < 4:
                                act.wait_ge(gu.sem, gu.at(e, m + 1))
                                act.wait_ge(hm.sem, hm.at(e, m + 1 - 2))
                                act.activation(SG[:, m % 2, :], ps[:, 2 + 2 * (m % 2), 0:SL],
                                               ACT.Silu).then_inc(silu.sem, 1)
                            if m < 3 and more:
                                split_w(e + 1, 1 - r, m)
                            if m == 4 and more:
                                for q in range(2):
                                    x_hi(e + 1, q)
                            if m >= 1:
                                h_hi(e, m - 1)
                        if more:
                            for q in range(2, NQ):
                                x_hi(e + 1, q)
                        for q in range(NQ):
                            act.wait_ge(yd.sem, yd.at(e, q + 1))
                            if q == 0 and stored is not None:
                                act.wait_ge(y_out, stored * (16 * ET))
                            act.copy(YS[:, 2 * q:2 * q + widths[q] // P, :],
                                     ps[:, 6 + q % 2, 0:2 * widths[q]].rearrange("p (t d) -> p t d", d=H)
                                     ).then_inc(ycp.sem, 1)

                    nc.scalar.preload_act_table_set("silu_and_others")
                    for k in range(3):
                        split_w(0, 0, k)
                    for q in range(NQ):
                        x_hi(0, q)
                    body(0, 0, True, None)
                    body(1, 1, True, 1)
                    with act.Fori(0, E // 2 - 2) as i:
                        body(i * 2 + 2, 0, True, i * 2 + 2)
                        body(i * 2 + 3, 1, True, i * 2 + 3)
                    body(E - 2, 0, True, E - 2)
                    body(E - 1, 1, False, E - 1)
                    act.wait_ge(y_out, E * 16 * ET)

                @block.vector
                def _(dve):
                    wlo.grant(dve)
                    xlo.grant(dve)
                    hm.grant(dve)
                    hlo.grant(dve)

                    def index(e, r):
                        dve.tensor_copy(IDX[:, r, :], INV[:, bass.ds(e * ET, ET)]).then_inc(idx.sem, 1)

                    def split_w(e, r, k):
                        dve.wait_ge(whi.sem, whi.at(e, k + 1))
                        w = slice(2 * k, 2 * k + 2)
                        dve.tensor_tensor(WS[:, r, 1, w], WRAW[:, w], WS[:, r, 0, w].bitcast(F32),
                                          ALU.subtract).then_inc(wlo.sem, 1)

                    def x_lo(e, q):
                        dve.wait_ge(xhi.sem, xhi.at(e, q + 1))
                        o = ps[:, q % 2, :].rearrange("p (a b) -> p a b", a=HC)[:, :, 0:widths[q]]
                        s = slice(2 * P * q, 2 * P * q + widths[q])
                        dve.tensor_tensor(XS[:, 1, :, s], o, XS[:, 0, :, s].bitcast(F32),
                                          ALU.subtract).then_inc(xlo.sem, 1)

                    def h_lo(e, m):
                        dve.wait_ge(hhi.sem, hhi.at(e, m + 1))
                        c, f = divmod(m, 2)
                        s = slice(SL * c, SL * c + SL)
                        dve.tensor_tensor(HS[:, 1, f, s], HF[:, m % 2, :], HS[:, 0, f, s].bitcast(F32),
                                          ALU.subtract).then_inc(hlo.sem, 1)

                    def gathered(e, r):
                        dve.wait_ge(xg_in[r], e * (8 * ET) + (2 - r) * 8 * ET)
                        apart(dve)

                    def body(e, r, more, ahead):
                        for m in range(5):
                            if m < 4:
                                dve.wait_ge(silu.sem, silu.at(e, m + 1))
                                dve.wait_ge(hlo.sem, hlo.at(e, m - 1))
                                dve.tensor_tensor(HF[:, m % 2, :], ps[:, 3 + 2 * (m % 2), 0:SL], SG[:, m % 2, :],
                                                  ALU.mult).then_inc(hm.sem, 1)
                            if m < 3 and more:
                                split_w(e + 1, 1 - r, m)
                            if m == 3:
                                dve.wait_ge(ycp.sem, ycp.at(e, 0))
                                apart(dve)
                                dve.tensor_copy(OIDX[:, r, :], DEST[:, bass.ds(e * ET, ET)]).then_inc(oidx.sem, 1)
                            if m == 0 and ahead:
                                gathered(e, r)
                                index(e + 2, r)
                            if m == 4 and more:
                                x_lo(e + 1, 0)
                            if m >= 1:
                                h_lo(e, m - 1)
                        if more:
                            for q in range(1, NQ):
                                x_lo(e + 1, q)

                    index(0, 0)
                    index(1, 1)
                    for k in range(3):
                        split_w(0, 0, k)
                    for q in range(NQ):
                        x_lo(0, q)

                    def pair(i, more):
                        body(i * 2, 0, True, more)
                        body(i * 2 + 1, 1, more, more)

                    with dve.Fori(0, E // 2 - 1) as i:
                        pair(i, True)
                    pair(E // 2 - 1, False)

                @block.tensor
                def _(pe):
                    turned.grant(pe)
                    gu.grant(pe)
                    yd.grant(pe)

                    def turn(e, r, quads):
                        if quads[0] == 0:
                            pe.wait_ge(xg_in[r], e * (8 * ET) + (2 - r) * 8 * ET)
                        for q in quads:
                            pe.wait_ge(xlo.sem, xlo.at(e, q + 1 - 2))
                            for j in range(widths[q] // P):
                                for h in range(HC):
                                    o = h * 2 * P + j * P
                                    ins = pe.transpose(ps[:, q % 2, o:o + P],
                                                       XG[:, r, 2 * q + j, h * P:(h + 1) * P], IDENT)
                            ins.then_inc(turned.sem, 1)

                    def product(dst, left, right):
                        terms = [(a, b, k) for k in range(HC) for a, b in ((0, 0), (0, 1), (1, 0))]
                        for n, (a, b, k) in enumerate(terms):
                            ins = pe.matmul(dst, left(a, k), right(b, k), start=(n == 0), stop=(n == len(terms) - 1))
                        return ins

                    def body(e, r, more):
                        pe.wait_ge(wlo.sem, wlo.at(e, 3))
                        pe.wait_ge(xlo.sem, xlo.at(e, NQ))
                        for m in range(4):
                            c, f = divmod(m, 2)
                            pe.wait_ge(hm.sem, hm.at(e, m + 1 - 2))
                            for n in range(2):
                                ins = product(
                                    ps[:, 2 + 2 * (m % 2) + n, 0:SL],
                                    lambda a, k: WS[:, r, a, 2 * n + k, f * P:(f + 1) * P],
                                    lambda b, k: XS[:, b, k, SL * c:SL * c + SL],
                                )
                            ins.then_inc(gu.sem, 1)
                        if more:
                            turn(e + 1, 1 - r, range(2))
                        for q in range(NQ):
                            if q == 1 and more:
                                turn(e + 1, 1 - r, range(2, NQ))
                            pe.wait_ge(hlo.sem, hlo.at(e, 2 * (2 * P * q + widths[q] > SL) + 2))
                            pe.wait_ge(ycp.sem, ycp.at(e, q + 1 - 2))
                            for j in range(widths[q] // P):
                                ins = product(
                                    ps[:, 6 + q % 2, j * H:(j + 1) * H],
                                    lambda a, k: HS[:, a, k, (2 * q + j) * P:(2 * q + j + 1) * P],
                                    lambda b, k: WS[:, r, b, 4 + k, :],
                                )
                            ins.then_inc(yd.sem, 1)

                    turn(0, 0, range(NQ))
                    loop(pe, body)


        class Combine:

            def __init__(self, stack, tag, ring, more):
                self.ring = ring
                self.gb = sb([P, TB], F32, stack, "gb")
                self.s1 = sb([P, TB], F32, stack, "s1")
                self.s2 = sb([P, TB], F32, stack, "s2")
                self.yg = sb([P, ring, CH, H], F32, stack, "yg")
                self.yg_in = [sem(f"{tag}_yg_in{r}") for r in range(ring)]
                self.comb = count(f"{tag}_combined", NC, ring)
                self.links = 2 + more
                self.ch = Chain(sem(f"{tag}_combine"), 1 + NC * self.links)

            def dve_begin(self, dve, a):
                self.ch.begin(a)
                b = bass.ds(TB * a, TB)
                dve.tensor_copy(self.gb[:], GATE[:, b])
                dve.tensor_scalar(self.s2[:], NMR[:, b], 0.5, None, ALU.mult)
                dve.tensor_scalar(self.s1[:], RSTD[:, b], 0.5, 1.0, ALU.mult, ALU.add).then_inc(self.ch.sem, 1)
                dve.wait_ge(self.ch.sem, self.ch.next())

            def load(self, eng, a, k):
                eng.wait_ge(self.comb.sem, self.comb.at(a, k + 1 - self.ring))
                apart(eng)
                rows = y_rows[0:T].rearrange("(k j p) d -> k p j d", p=P, j=CH)
                eng.dma_start(self.yg[:, k % self.ring], rows[a * NC + k]).then_inc(self.yg_in[k % self.ring], 16)

            def dve_scale(self, dve, a, k):
                for j in range(CH):
                    c = CH * k + j
                    x_t = X[:, TB * a + c, :]
                    ins = dve.tensor_scalar(x_t, x_t, self.s1[:, c:c + 1], self.s2[:, c:c + 1], ALU.mult, ALU.add)
                ins.then_inc(self.ch.sem, 1)

            def dve_add(self, dve, a, k):
                dve.wait_ge(self.ch.sem, self.ch.at(a, 1 + k * self.links + 1))
                dve.wait_ge(self.yg_in[k % self.ring],
                            a * (16 * NC // self.ring) + 16 * (k // self.ring + 1))
                for j in range(CH):
                    c = CH * k + j
                    x_t = X[:, TB * a + c, :]
                    ins = dve.scalar_tensor_tensor(x_t, self.yg[:, k % self.ring, j, :], self.gb[:, c:c + 1], x_t,
                                                   ALU.mult, ALU.add)
                ins.then_inc(self.ch.sem, 1)

            def dve_added(self, dve, a, k):
                dve.wait_ge(self.ch.sem, self.ch.at(a, 1 + k * self.links + 2))
                dve.sem_inc(self.comb.sem, 1)

        def attention():
            with ExitStack() as st:
                BG, BX, BY = 0, 1, 3
                BZ = (2, 6)
                tail = Tail(st, "p3", (4, 5, 4, 7), 1, 2)
                comb = Combine(st, "p3", 2, 1)
                s = lambda shape, dt=F32, name="a": sb(shape, dt, st, name)
                WA = s([P, 8, H], F32R)
                WC, WCT = s([P, HC, H]), s([P, HC, H])
                VEC = s([P, 6, HC])
                A1, B1, BD, NBD, ABD = (VEC[:, k, :] for k in range(5))
                RA, NA, RB, NB = s([P, TB]), s([P, TB]), s([P, TB]), s([P, TB])
                BSA, MVA, MRA, VEA = s([P, 2, CH, 6]), s([P, 2, CH, 2]), s([P, CH]), s([P, CH])
                XA = s([P, 2, CH, H + 1])
                XB = s([P, 2, CH, H])
                XS = s([P, 3, 2, HC, CT], F32R)
                AB = s([P, 2, HC, CT])
                CC = s([P, 2, HC, CT])
                YT = s([P, 2, HC, CT])
                DIAG = s([P, 2, HC, P])
                NG = H + 1 + P + 1
                GS = s([P, NG])
                UV = s([P, 5, HC])
                s_w, s_set = sem("p3_w_in"), sem("p3_setup")
                stats = count("a_stats", NC)
                rstd = count("a_rstd", NC, 2)
                normed = count("a_normed", NC, 1)
                gram_done = count("a_gram", NC, 2)
                gram_read = count("a_gram_read", 2, 1)
                sums_done = count("a_sums", 1)
                b_normed = count("b_norm", NC)
                b_turned = count("b_turned", NC, 2)
                x_hi_done = count("b_hi", NC)
                x_lo_done = count("b_lo", NC, 1)
                z_done = count("b_z", NC)
                log_done = count("b_log", NC)
                softplus_done = count("b_softplus", NC, 2)
                scanned = count("b_scan", NC, 2)
                da_done = count("b_da", NC, 2)
                diag = count("a_diagonals", 1)
                residual_done = count("b_residual", NC, 2)
                x_added = count("b_x", NC, 1)
                a_chain = Chain(sem("a_pool"), 3 * NC)
                b_chain = Chain(sem("b_dve"), 4)
                log_chain = Chain(sem("b_act"), 2 * NC)
                block = st.enter_context(nc.Block())
                MID = BATCH - 2

                STEPS = NC + 2
                LAST_LAG = 5
                A_AT = (1, 2, 3, 4, 5, 6, 7, 8)
                POST_AT = (4, 5, 5, 6, 7, 8, 9)
                INV_AT = (7, 8, 9, 9)

                def a_at(s):
                    return [k for k in range(NC) if A_AT[k] == s]

                def stage(f, s, lag, t, prev):
                    if t is not None and 0 <= s - lag < NC:
                        f(t, s - lag)
                    elif prev is not None and 0 <= s - lag + STEPS < NC:
                        f(prev, s - lag + STEPS)

                def turns(eng, body, last):
                    body(0, None, 1, STEPS)
                    with eng.Fori(0, MID) as i:
                        body(i + 1, i, i + 2, STEPS)
                    body(BATCH - 1, BATCH - 2, None, STEPS)
                    body(None, BATCH - 1, None, NC + LAST_LAG - STEPS)
                    last()

                @block.sync
                def _(sp):
                    tail.sp_setup()
                    sp.dma_start(WA[:].bitcast(F32).rearrange("p a b -> p (a b)"), w_ready).then_inc(s_w, 16)
                    for dst, src in ((WC, w_c), (WCT, w_c_t)):
                        sp.dma_start(dst[:], src.rearrange("(a p) e -> p a e", p=P)).then_inc(s_w, 16)
                    for k, v in enumerate((a_vec, b_vec, b_delta)):
                        sp.dma_start(VEC[:, k, :], v).then_inc(s_w, 16)
                    with sp.Fori(0, BATCH) as t:
                        for c in range(NC):
                            tail.sp_store(sp, t, c)

                @block.gpsimd
                def _(pool):
                    tail.pool_setup()
                    rstd.grant(pool)

                    def a_rstd(a, k):
                        if k == 0:
                            a_chain.begin(a)
                            pool.wait_ge(normed.sem, normed.at(a, 0))
                        pool.wait_ge(stats.sem, stats.at(a, k + 1))
                        apart(pool)
                        c = slice(CH * k, CH * k + CH)
                        mean, var = MVA[:, k % 2, :, 0], MVA[:, k % 2, :, 1]
                        nc.gpsimd.tensor_scalar(VEA[:], var, EPS, None, ALU.add).then_inc(a_chain.sem, 1)
                        pool.wait_ge(a_chain.sem, a_chain.next())
                        nc.gpsimd.tensor_tensor(RA[:, c], VEA[:], NHALF, ALU.pow).then_inc(a_chain.sem, 1)
                        pool.wait_ge(a_chain.sem, a_chain.next())
                        nc.gpsimd.tensor_tensor(MRA[:], mean, RA[:, c], ALU.mult).then_inc(a_chain.sem, 1)
                        pool.wait_ge(a_chain.sem, a_chain.next())
                        apart(pool)
                        nc.gpsimd.tensor_scalar(NA[:, c], MRA[:], -1.0, None, ALU.mult).then_inc(rstd.sem, 1)

                    def body(t, prev, a, steps):
                        if a is not None:
                            for k in range(2):
                                comb.load(pool, a, k)
                        for s in range(steps):
                            if a is not None:
                                for k in a_at(s):
                                    a_rstd(a, k)
                                    if k + 2 < NC:
                                        comb.load(pool, a, k + 2)
                            stage(lambda b, c: tail.pool_rstd(pool, b, c), s, 3, t, prev)

                    for k in range(2):
                        comb.load(pool, 0, k)
                    for k in range(NC):
                        a_rstd(0, k)
                        if k + 2 < NC:
                            comb.load(pool, 0, k + 2)
                    turns(pool, body, lambda: None)

                @block.scalar
                def _(act):
                    tail.act_setup(act)
                    normed.grant(act)
                    da_done.grant(act)
                    act.wait_ge(s_w, 96)
                    act.wait_ge(s_set, 2)

                    def a_norm(a, k):
                        act.wait_ge(gram_done.sem, gram_done.at(a, k - 1))
                        act.wait_ge(rstd.sem, rstd.at(a, k + 1))
                        apart(act)
                        for j in range(CH):
                            c = CH * k + j
                            ins = act.activation(XA[:, k % 2, j, 0:H], X[:, TB * a + c, :], ACT.Identity,
                                                 bias=NA[:, c:c + 1], scale=RA[:, c:c + 1])
                        ins.then_inc(normed.sem, 1)

                    def b_norm(t, s):
                        act.wait_ge(b_turned.sem, b_turned.at(t, s - 1))
                        act.wait_ge(b_chain.sem, b_chain.at(t, 1))
                        apart(act)
                        for j in range(CH):
                            c = CH * s + j
                            ins = act.activation(XB[:, s % 2, j, :], X[:, TB * t + c, :], ACT.Identity,
                                                 bias=NB[:, c:c + 1], scale=RB[:, c:c + 1])
                        ins.then_inc(b_normed.sem, 1)

                    def x_hi(t, s):
                        act.wait_ge(b_turned.sem, b_turned.at(t, s + 1))
                        act.wait_ge(residual_done.sem, residual_done.at(t, (-1, 0, 0)[s] if s < 3 else s - 2))
                        act.copy(XS[:, s % 3, 0].rearrange("p a b -> p (a b)"), ps[:, BX, :]).then_inc(x_hi_done.sem, 1)

                    def softplus(t, s):
                        log_chain.begin(t, 2 * s)
                        act.wait_ge(z_done.sem, z_done.at(t, s + 1))
                        act.wait_ge(scanned.sem, scanned.at(t, s - 1))
                        act.wait_ge(da_done.sem, da_done.at(t, s - 1))
                        for h in range(HC):
                            ins = act.activation(AB[:, s % 2, h, :], ps[:, BZ[s % 2], h * CT:(h + 1) * CT], ACT.Abs,
                                                 bias=BD[:, h:h + 1])
                        ins.then_inc(log_chain.sem, 1)
                        act.wait_ge(log_chain.sem, log_chain.next())
                        act.activation(AB[:, s % 2], AB[:, s % 2], ACT.Exp, scale=-1.0).then_inc(log_chain.sem, 1)
                        act.wait_ge(log_chain.sem, log_chain.next())
                        act.activation(AB[:, s % 2], AB[:, s % 2], ACT.Ln, bias=1.0).then_inc(log_done.sem, 1)

                    def d_a(t, s):
                        act.wait_ge(softplus_done.sem, softplus_done.at(t, s + 1))
                        act.wait_ge(residual_done.sem, residual_done.at(t, s - 1))
                        for h in range(HC):
                            ins = act.activation(YT[:, s % 2, h, :], AB[:, s % 2, h, :], ACT.Exp,
                                                 bias=ABD[:, h:h + 1], scale=A1[:, h:h + 1])
                        ins.then_inc(da_done.sem, 1)

                    def body(t, prev, a, steps):
                        for s in range(steps):
                            if t is not None and s == 0:
                                b_norm(t, 0)
                            stage(d_a, s, 2, t, prev)
                            stage(x_hi, s, 0, t, prev)
                            if t is not None and prev is not None and s == POST_AT[0] + 1:
                                tail.act_exp(act, prev)
                            stage(lambda b, c: tail.act_norm(act, b, c), s, 4, t, prev)
                            if t is not None and s < NC - 1:
                                b_norm(t, s + 1)
                            stage(softplus, s, 1, t, prev)
                            stage(lambda b, c: tail.act_evac(act, b, c), s, 4, t, prev)
                            if a is not None:
                                for k in a_at(s):
                                    a_norm(a, k)

                    nc.scalar.preload_act_table_set("natural_log_exp_and_others")
                    for k in range(NC):
                        a_norm(0, k)
                    turns(act, body, lambda: tail.act_exp(act, BATCH - 1))

                @block.vector
                def _(dve):
                    for c in (gram_read, x_lo_done, softplus_done, scanned, x_added, comb.comb):
                        c.grant(dve)
                    tail.dve_setup()
                    dve.memset(XA[:, :, :, H:H + 1], 1.0)
                    dve.wait_ge(s_w, 96)
                    dve.tensor_scalar(NBD, BD, -1.0, None, ALU.mult).then_inc(s_set, 1)
                    dve.tensor_tensor(ABD, A1, BD, ALU.mult).then_inc(s_set, 1)
                    dve.wait_ge(s_set, 2)

                    def a_stats(a, k):
                        comb.dve_added(dve, a, k)
                        for j in range(CH):
                            ins = dve.bn_stats(BSA[:, k % 2, j, :], X[:, TB * a + (CH * k + j), :])
                        ins.then_inc(comb.ch.sem, 1)

                    def a_aggr(a, k):
                        dve.wait_ge(rstd.sem, rstd.at(a, k - 1))
                        dve.wait_ge(comb.ch.sem, comb.ch.at(a, 1 + k * comb.links + 3))
                        apart(dve)
                        for j in range(CH):
                            ins = dve.bn_aggr(MVA[:, k % 2, j, :], BSA[:, k % 2, j, :])
                        ins.then_inc(stats.sem, 1)

                    def a_chunk(a, k):
                        comb.dve_scale(dve, a, k)
                        comb.dve_add(dve, a, k)
                        a_stats(a, k)
                        a_aggr(a, k)

                    def a_sums(a):
                        dve.wait_ge(gram_done.sem, gram_done.at(a, NC))
                        dve.tensor_copy(GS[:], ps[:, BG, 0:NG]).then_inc(gram_read.sem, 1)

                    def a_factors(a):
                        dve.wait_ge(sums_done.sem, sums_done.at(a, 1))
                        dve.wait_ge(residual_done.sem, residual_done.at(a, 0))
                        sums = ps[:, BG, :]
                        scratch = DIAG[:].rearrange("p a b c -> p (a b c)")
                        for n, (l, r) in enumerate(((WC[:, 0, :], GS[:, 0:H]), (WC[:, 1, 0:P], sums[:, 0:P]),
                                                    (WC[:, 1, P:H], GS[:, H + 1:H + 1 + P]))):
                            o = (0, H, H + P)[n]
                            ins = dve.tensor_tensor_reduce(out=scratch[:, o:o + l.shape[1]], in0=l, in1=r, scale=1.0,
                                                           scalar=0.0, op0=ALU.mult, op1=ALU.add,
                                                           accum_out=UV[:, 2 + n // 2, n % 2:n % 2 + 1])
                        ins.then_inc(b_chain.sem, 1)
                        dve.wait_ge(b_chain.sem, b_chain.next())
                        dve.tensor_tensor(UV[:, 2, 1:2], UV[:, 2, 1:2], UV[:, 3, 0:1], ALU.add).then_inc(b_chain.sem, 1)
                        dve.wait_ge(b_chain.sem, b_chain.next())
                        dve.tensor_tensor(UV[:, 0, :], UV[:, 2, :], B1, ALU.mult)
                        dve.tensor_tensor(UV[:, 1, :], sums[:, P:P + HC], B1, ALU.mult).then_inc(b_chain.sem, 1)
                        dve.wait_ge(b_chain.sem, b_chain.next())
                        dve.sem_inc(gram_read.sem, 1)
                        for n in range(2):
                            for h in range(HC):
                                ins = dve.tensor_scalar(DIAG[:, n, h, :], IDENT, UV[:, n, h:h + 1], None, ALU.mult)
                        ins.then_inc(diag.sem, 1)

                    def x_lo(t, s):
                        dve.wait_ge(x_hi_done.sem, x_hi_done.at(t, s + 1))
                        dve.tensor_tensor(XS[:, s % 3, 1].rearrange("p a b -> p (a b)"), ps[:, BX, :],
                                          XS[:, s % 3, 0].bitcast(F32).rearrange("p a b -> p (a b)"),
                                          ALU.subtract).then_inc(x_lo_done.sem, 1)

                    def softplus(t, s):
                        dve.wait_ge(log_done.sem, log_done.at(t, s + 1))
                        for h in range(HC):
                            ins = dve.scalar_tensor_tensor(AB[:, s % 2, h, :], ps[:, BZ[s % 2], h * CT:(h + 1) * CT],
                                                           NBD[:, h:h + 1], AB[:, s % 2, h, :], ALU.max, ALU.add)
                        ins.then_inc(softplus_done.sem, 1)

                    def scan(t, s):
                        dve.wait_ge(softplus_done.sem, softplus_done.at(t, s + 1))
                        dve.wait_ge(scanned.sem, scanned.at(t, s))
                        dve.wait_ge(residual_done.sem, residual_done.at(t, s - 1))
                        for h in range(HC):
                            start = 0.0 if s == 0 else CC[:, 1 - s % 2, h, CT - 1:CT]
                            ins = dve.tensor_tensor_scan(CC[:, s % 2, h, :], BD[:, h:h + 1].to_broadcast([P, CT]),
                                                         AB[:, s % 2, h, :], start, ALU.add, ALU.add)
                        ins.then_inc(scanned.sem, 1)

                    def x_new(t, s):
                        dve.wait_ge(residual_done.sem, residual_done.at(t, s + 1))
                        x_t = X[:, bass.ds(TB * t + CH * s, CH), :].rearrange("p a b -> p (a b)")
                        dve.tensor_tensor(x_t, x_t, ps[:, BY, :], ALU.add).then_inc(x_added.sem, 1)

                    def x_stats(t, s):
                        dve.wait_ge(x_added.sem, x_added.at(t, s + 1))
                        apart(dve)
                        tail.dve_stats(dve, t, s)

                    def x_aggr(t, s):
                        tail.dve_aggr(dve, t, s)

                    def body(t, prev, a, steps):
                        if t is not None:
                            b_chain.begin(t)
                            dve.wait_ge(rstd.sem, rstd.at(t, NC))
                            dve.tensor_copy(RB[:], RA[:])
                            dve.tensor_copy(NB[:], NA[:]).then_inc(b_chain.sem, 1)
                            dve.wait_ge(b_chain.sem, b_chain.next())
                        if a is not None:
                            comb.dve_begin(dve, a)
                        for s in range(steps):
                            chunks = a_at(s) if a is not None else []
                            head = chunks[0:1]
                            stage(x_lo, s, 1, t, prev)
                            for k in head:
                                comb.dve_scale(dve, a, k)
                            if t is not None and s == 1:
                                a_sums(t)
                            if t is not None and s == 2:
                                a_factors(t)
                            stage(softplus, s, 2, t, prev)
                            for k in head:
                                comb.dve_add(dve, a, k)
                            stage(scan, s, 2, t, prev)
                            for k in head:
                                a_stats(a, k)
                            stage(x_new, s, 3, t, prev)
                            for k in head:
                                a_aggr(a, k)
                            stage(x_stats, s, 3, t, prev)
                            for k in chunks[1:]:
                                comb.dve_scale(dve, a, k)
                            stage(x_aggr, s, 3, t, prev)
                            for k in chunks[1:]:
                                comb.dve_add(dve, a, k)
                                a_stats(a, k)
                                a_aggr(a, k)
                            if prev is not None and s == 2:
                                tail.dve_keep(dve, prev)
                            if t is not None and prev is not None:
                                for q in range(7):
                                    if POST_AT[q] == s:
                                        tail.post(dve, prev, q)
                        if t is not None:
                            b_chain.end()

                    comb.dve_begin(dve, 0)
                    for k in range(NC):
                        a_chunk(0, k)

                    def rest():
                        for k in range(7):
                            tail.post(dve, BATCH - 1, k)
                        tail.dve_finish(dve)

                    turns(dve, body, rest)

                @block.tensor
                def _(pe):
                    tail.pe_setup(pe)
                    for c in (gram_done, b_turned, residual_done):
                        c.grant(pe)
                    pe.wait_ge(s_w, 96)

                    def gram(a, k):
                        pe.wait_ge(normed.sem, normed.at(a, k + 1))
                        if k == 0:
                            pe.wait_ge(gram_read.sem, gram_read.at(a, 0))
                        for j in range(CH):
                            x_c = XA[:, k % 2, j, :]
                            first = k == 0 and j == 0
                            end = k == NC - 1 and j == CH - 1
                            pe.matmul(ps[:, BG, 0:H + 1], x_c[:, 0:P], x_c, start=first, stop=end,
                                      skip_group_check=True)
                            ins = pe.matmul(ps[:, BG, H + 1:NG], x_c[:, P:H], x_c[:, P:H + 1], start=False, stop=end,
                                            skip_group_check=True)
                        ins.then_inc(gram_done.sem, 1)

                    def sums(a):
                        pe.wait_ge(gram_read.sem, gram_read.at(a, 1))
                        pe.transpose(ps[:, BG, 0:P], GS[:, P:H], IDENT)
                        for h in range(HC):
                            for k in range(HC):
                                ins = pe.matmul(ps[:, BG, P + h:P + h + 1], WCT[:, k, h * P:(h + 1) * P],
                                                GS[:, (H, NG - 1)[k]:(H, NG - 1)[k] + 1], start=(k == 0),
                                                stop=(k == HC - 1))
                        ins.then_inc(sums_done.sem, 1)

                    def turn(t, s):
                        pe.wait_ge(b_normed.sem, b_normed.at(t, s + 1))
                        pe.wait_ge(x_lo_done.sem, x_lo_done.at(t, s))
                        for h in range(HC):
                            for j in range(CH):
                                o = h * CT + j * P
                                ins = pe.transpose(ps[:, BX, o:o + P], XB[:, s % 2, j, h * P:(h + 1) * P], IDENT)
                        ins.then_inc(b_turned.sem, 1)

                    terms = [(a, b, k) for k in range(HC) for a, b in ((0, 0), (0, 1), (1, 0))]

                    def delta(t, s):
                        pe.wait_ge(x_lo_done.sem, x_lo_done.at(t, s + 1))
                        pe.wait_ge(softplus_done.sem, softplus_done.at(t, s - 1))
                        for h in range(HC):
                            for n, (a, b, k) in enumerate(terms):
                                ins = pe.matmul(ps[:, BZ[s % 2], h * CT:(h + 1) * CT],
                                                WA[:, 2 * a + k, h * P:(h + 1) * P], XS[:, s % 3, b, k, :],
                                                start=(n == 0), stop=(n == len(terms) - 1))
                        ins.then_inc(z_done.sem, 1)

                    def residual(t, s):
                        if s == 0:
                            pe.wait_ge(diag.sem, diag.at(t, 1))
                        pe.wait_ge(da_done.sem, da_done.at(t, s + 1))
                        pe.wait_ge(scanned.sem, scanned.at(t, s + 1))
                        pe.wait_ge(x_added.sem, x_added.at(t, s))
                        for j in range(CH):
                            for n, (a, b, k) in enumerate(terms):
                                pe.matmul(ps[:, BY, j * H:(j + 1) * H], XS[:, s % 3, a, k, j * P:(j + 1) * P],
                                          WA[:, 4 + 2 * b + k, :], start=(n == 0), stop=False, skip_group_check=True)
                            for n, src in enumerate((YT, CC)):
                                for h in range(HC):
                                    ins = pe.matmul(ps[:, BY, j * H + h * P:j * H + (h + 1) * P],
                                                    src[:, s % 2, h, j * P:(j + 1) * P], DIAG[:, n, h, :],
                                                    start=False, stop=(n == 1 and h == HC - 1),
                                                    skip_group_check=True)
                        ins.then_inc(residual_done.sem, 1)

                    def body(t, prev, a, steps):
                        post = t is not None and prev is not None
                        for s in range(steps):
                            stage(residual, s, 3, t, prev)
                            stage(turn, s, 0, t, prev)
                            if t is not None and s == 1:
                                sums(t)
                            stage(delta, s, 1, t, prev)
                            if post and s == POST_AT[0] + 1:
                                pe.wait_ge(tail.evac.sem, tail.evac.at(t, s - 4))
                                tail.pe_count(pe, prev)
                            stage(lambda b, c: tail.pe_logits(pe, b, c), s, 5, t, prev)
                            if post and s == POST_AT[0] + 1:
                                pe.wait_ge(tail.cread.sem, tail.cread.at(prev, 1))
                            stage(lambda b, c: tail.pe_turn(pe, b, c), s, 4, t, prev)
                            if a is not None:
                                for k in a_at(s - 1):
                                    gram(a, k)
                            if post:
                                for q in range(4):
                                    if INV_AT[q] == s:
                                        tail.pe_inv(pe, prev, q)

                    for k in range(NC):
                        gram(0, k)

                    def rest():
                        tail.pe_count(pe, BATCH - 1)
                        for q in range(4):
                            tail.pe_inv(pe, BATCH - 1, q)
                        tail.pe_finish(pe)

                    turns(pe, body, rest)

        def finish():
            with ExitStack() as st:
                comb = Combine(st, "p5", 8, 0)
                s_out = sem("out_stored")
                block = st.enter_context(nc.Block())
                rows = out.rearrange("(b k j p) d -> b k p j d", p=P, j=CH, k=NC)

                @block.sync
                def _(sp):
                    with sp.Fori(0, BATCH) as a:
                        for k in range(NC):
                            sp.wait_ge(comb.comb.sem, comb.comb.at(a, k + 1))
                            sp.dma_start(rows[a, k], X[:, bass.ds(TB * a + CH * k, CH), :]).then_inc(s_out, 16)
                    sp.wait_ge(s_out, 16 * BATCH * NC)

                @block.scalar
                def _(act):
                    with act.Fori(0, BATCH) as a:
                        for k in range(NC):
                            comb.load(act, a, k)

                @block.vector
                def _(dve):
                    comb.comb.grant(dve)

                    with dve.Fori(0, BATCH) as a:
                        comb.dve_begin(dve, a)
                        for k in range(NC + 1):
                            if k < NC:
                                comb.dve_scale(dve, a, k)
                            if k >= 1:
                                comb.dve_added(dve, a, k - 1)
                            if k < NC:
                                comb.dve_add(dve, a, k)

        experts("p2")
        attention()
        experts("p4")
        finish()


_ARRAYS = ["x", "w_proj0", "w_delta_t", "w_c", "w_c_t", "w_r_t", "a_vec", "b_vec", "d_vec", "b_delta",
           "w_router", "w_gate", "w_up", "w_down", "c_f32", "c_bf16"]


def kernel(L0_attn_x, L0_attn_W_proj, L0_attn_A, L0_attn_Bp, L0_attn_D, L0_attn_W_delta, L0_attn_b_delta,
           L0_ffn_w_router, L0_ffn_w_gate, L0_ffn_w_up, L0_ffn_w_down):
    import concourse.bacc as bacc
    import ml_dtypes
    import numpy as np
    from concourse.bass_utils import run_bass_kernel_spmd

    def c(a):
        return np.ascontiguousarray(a)

    def halves(v):
        return c(np.asarray(v).reshape(HC, P).T)

    w = np.asarray(L0_attn_W_proj)
    i, f = np.arange(P), np.float32
    c_f32 = np.concatenate([np.eye(P, dtype=f), np.tile((E - np.arange(E)).astype(f), (P, 1)),
                            i[:, None].astype(f), np.tile(np.arange(TB).astype(f), (P, 1)),
                            np.full((P, CH), -0.5, f)], axis=1)
    c_bf16 = np.concatenate([(i[:, None] <= i[None, :]).astype(f), np.ones((P, P), f), np.tile(i.astype(f), (P, 1)),
                             np.tile(np.arange(ST).astype(f), (P, 1)), np.zeros((P, P), f)],
                            axis=1).astype(ml_dtypes.bfloat16)
    arrays = dict(
        x=c(np.asarray(L0_attn_x).reshape(T, H)), w_proj0=c(w[0:H]), w_delta_t=c(np.asarray(L0_attn_W_delta).T),
        w_c=c(w[2 * H:3 * H]), w_c_t=c(w[2 * H:3 * H].T), w_r_t=c(w[3 * H:4 * H].T), a_vec=halves(L0_attn_A),
        b_vec=halves(L0_attn_Bp), d_vec=c(np.broadcast_to(np.asarray(L0_attn_D).reshape(1, 1), (P, 1))),
        b_delta=halves(L0_attn_b_delta), w_router=c(L0_ffn_w_router), w_gate=c(L0_ffn_w_gate),
        w_up=c(L0_ffn_w_up), w_down=c(L0_ffn_w_down), c_f32=c_f32, c_bf16=c_bf16)
    nc = bacc.Bacc("TRN2", target_bir_lowering=False, num_devices=1)
    feeds, args = {}, []
    for name in _ARRAYS:
        a = arrays[name]
        feeds[f"in_{name}"] = a
        args.append(nc.dram_tensor(f"in_{name}", a.shape, mybir.dt.from_np(a.dtype), kind="ExternalInput").ap())
    out = nc.dram_tensor("out", [T, H], F32, kind="ExternalOutput").ap()
    macaron(nc, *args, out)
    r = run_bass_kernel_spmd(nc, [feeds], core_ids=[0])
    return r.results[0]["out"].reshape(BATCH, SEQ, H)
```
